# Optimizing a Trainium2 kernel written in Bass

```python
import numpy as np
import jax
import jax.numpy as jnp

def _softmax(x, axis=-1):
    return jax.nn.softmax(x, axis=axis)

def _gelu(x):
    return jax.nn.gelu(x, approximate=True)

def _silu(x):
    return jax.nn.silu(x)

def _sigmoid(x):
    return jax.nn.sigmoid(x)

def _layernorm(x, axis=-1, eps=1e-05):
    m = jnp.mean(x, axis=axis, keepdims=True)
    v = jnp.var(x, axis=axis, keepdims=True)
    return (x - m) / jnp.sqrt(v + eps)

def _scatter_add(tgt, idx, src, axis=0):
    return tgt.at[idx].add(src)

def _segment_sum(src, seg, n):
    return jax.ops.segment_sum(src, seg, n)
kernel_name = 'mk_audio_tower_d1_tok_audfeat256_r4_088b6a'

def setup_inputs(seed: int=0):
    np.random.seed(seed)
    _w = jnp.asarray

    def _rec_inputs():
        import jax
        import jax.numpy as jnp
        _rk = jax.random.key(seed)
        x = -9.80646e-05 + 1.00041 * jax.random.normal(jax.random.fold_in(_rk, 1), (16, 4, 375), jnp.float32)
        return x
    x = _rec_inputs()

    def _L0_tok_setup():
        import jax, jax.numpy as jnp
        from jax import lax
        import numpy as np
        NUM_BLOCKS = 9
        KERNEL = 3
        BN_EPS = 1e-05

        def _conv1d(x, w, padding, dilation):
            return lax.conv_general_dilated(x, w, window_strides=(1,), padding=[(padding, padding)], rhs_dilation=(dilation,), dimension_numbers=('NCH', 'OIH', 'NCH'))
        key = jax.random.key(seed)
        ks = jax.random.split(key, 8)
        B, C, L, V = (32, 4, 1024, 64)
        x = jax.random.normal(ks[0], (B, C, L), dtype=jnp.float32)
        conv_w = jax.random.normal(ks[1], (NUM_BLOCKS, C, C, KERNEL), dtype=jnp.float32) * 0.3
        conv_b = jax.random.normal(ks[2], (NUM_BLOCKS, C), dtype=jnp.float32) * 0.1
        bn_gamma = jnp.ones((NUM_BLOCKS, C), dtype=jnp.float32)
        bn_beta = jnp.zeros((NUM_BLOCKS, C), dtype=jnp.float32)
        bn_mean = jax.random.normal(ks[3], (NUM_BLOCKS, C), dtype=jnp.float32) * 0.1
        bn_var = jax.random.uniform(ks[4], (NUM_BLOCKS, C), dtype=jnp.float32, minval=0.5, maxval=1.5)
        out_w = jax.random.normal(ks[5], (V, C, 1), dtype=jnp.float32) * 0.3
        out_b = jax.random.normal(ks[6], (V,), dtype=jnp.float32) * 0.1
        return {'x': x, 'conv_w': conv_w, 'conv_b': conv_b, 'bn_gamma': bn_gamma, 'bn_beta': bn_beta, 'bn_mean': bn_mean, 'bn_var': bn_var, 'out_w': out_w, 'out_b': out_b}
    _L0_tok_all = _L0_tok_setup()
    _L0_tok_in = {k: v for k, v in _L0_tok_all.items() if k in ('conv_w', 'conv_b', 'bn_gamma', 'bn_beta', 'bn_mean', 'bn_var', 'out_w', 'out_b')}
    del _L0_tok_all

    def _L0_attn_setup():
        import jax, jax.numpy as jnp
        import numpy as np
        H, D = (8, 32)
        EPS = 1e-05
        key = jax.random.key(seed)
        ks = jax.random.split(key, 4)
        B, N, C = (2, 512, 64)
        inner = H * D
        return {'node_features': jax.random.normal(ks[0], (B, N, C), jnp.float32), 'ln_gamma': jnp.ones((C,), jnp.float32), 'ln_beta': jnp.zeros((C,), jnp.float32), 'W_qkv': jax.random.normal(ks[1], (3 * inner, C), jnp.float32) * 0.02, 'W_gate': jax.random.normal(ks[2], (inner, C), jnp.float32) * 0.02, 'b_gate': jnp.ones((inner,), jnp.float32), 'W_final': jax.random.normal(ks[3], (C, inner), jnp.float32) * 0.02, 'b_final': jnp.zeros((C,), jnp.float32)}
    _L0_attn_all = _L0_attn_setup()
    _L0_attn_in = {k: v for k, v in _L0_attn_all.items() if k in ('ln_gamma', 'ln_beta', 'W_qkv', 'W_gate', 'b_gate', 'W_final', 'b_final')}
    del _L0_attn_all

    def _L0_ffn_setup():
        import jax, jax.numpy as jnp
        import numpy as np
        B, H, E, IN, OUT = (1024, 1, 8, 64, 64)

        @jax.custom_vjp
        def bin_active(x):
            return jnp.sign(x)

        def _ba_fwd(x):
            return (jnp.sign(x), x)

        def _ba_bwd(x, g):
            return (g * (jnp.abs(x) <= 1.0).astype(g.dtype),)
        bin_active.defvjp(_ba_fwd, _ba_bwd)

        @jax.custom_vjp
        def bin_gate(x):
            return (x > 0.5).astype(x.dtype)

        def _bg_fwd(x):
            return ((x > 0.5).astype(x.dtype), None)

        def _bg_bwd(_, g):
            return (g,)
        bin_gate.defvjp(_bg_fwd, _bg_bwd)
        key = jax.random.key(seed)
        k1, k2, k3, k4, k5 = jax.random.split(key, 5)
        x = jax.random.normal(k1, (B, H, IN), dtype=jnp.float32)
        weight = jax.random.normal(k2, (H, E, IN, OUT), dtype=jnp.float32) * 0.05
        proj_w = jax.random.normal(k3, (E, IN), dtype=jnp.float32) * 0.05
        proj_b = jax.random.normal(k4, (E,), dtype=jnp.float32) * 0.05
        scale = jax.random.normal(k5, (H, 1, OUT), dtype=jnp.float32) * 0.1
        return {'x': x, 'weight': weight, 'proj_w': proj_w, 'proj_b': proj_b, 'scale': scale}
    _L0_ffn_all = _L0_ffn_setup()
    _L0_ffn_in = {k: v for k, v in _L0_ffn_all.items() if k in ('weight', 'proj_w', 'proj_b', 'scale')}
    del _L0_ffn_all
    return {'x': x, 'L0_tok_conv_w': _L0_tok_in['conv_w'], 'L0_tok_conv_b': _L0_tok_in['conv_b'], 'L0_tok_bn_gamma': _L0_tok_in['bn_gamma'], 'L0_tok_bn_beta': _L0_tok_in['bn_beta'], 'L0_tok_bn_mean': _L0_tok_in['bn_mean'], 'L0_tok_bn_var': _L0_tok_in['bn_var'], 'L0_tok_out_w': _L0_tok_in['out_w'], 'L0_tok_out_b': _L0_tok_in['out_b'], 'L0_attn_ln_gamma': _L0_attn_in['ln_gamma'], 'L0_attn_ln_beta': _L0_attn_in['ln_beta'], 'L0_attn_W_qkv': _L0_attn_in['W_qkv'], 'L0_attn_W_gate': _L0_attn_in['W_gate'], 'L0_attn_b_gate': _L0_attn_in['b_gate'], 'L0_attn_W_final': _L0_attn_in['W_final'], 'L0_attn_b_final': _L0_attn_in['b_final'], 'L0_ffn_weight': _L0_ffn_in['weight'], 'L0_ffn_proj_w': _L0_ffn_in['proj_w'], 'L0_ffn_proj_b': _L0_ffn_in['proj_b'], 'L0_ffn_scale': _L0_ffn_in['scale']}

def reference(x, L0_tok_conv_w, L0_tok_conv_b, L0_tok_bn_gamma, L0_tok_bn_beta, L0_tok_bn_mean, L0_tok_bn_var, L0_tok_out_w, L0_tok_out_b, L0_attn_ln_gamma, L0_attn_ln_beta, L0_attn_W_qkv, L0_attn_W_gate, L0_attn_b_gate, L0_attn_W_final, L0_attn_b_final, L0_ffn_weight, L0_ffn_proj_w, L0_ffn_proj_b, L0_ffn_scale):
    import jax
    import jax.numpy as jnp

    def _L0_tok_ref(x, conv_w, conv_b, bn_gamma, bn_beta, bn_mean, bn_var, out_w, out_b):
        import jax, jax.numpy as jnp
        from jax import lax
        import numpy as np
        NUM_BLOCKS = 9
        KERNEL = 3
        BN_EPS = 1e-05

        def _conv1d(x, w, padding, dilation):
            return lax.conv_general_dilated(x, w, window_strides=(1,), padding=[(padding, padding)], rhs_dilation=(dilation,), dimension_numbers=('NCH', 'OIH', 'NCH'))
        L = x.shape[-1]
        for i in range(NUM_BLOCKS):
            dilation = 2 ** i
            pad = (KERNEL - 1) * dilation
            residual = x
            h = _conv1d(x, conv_w[i], pad, dilation) + conv_b[i][None, :, None]
            h = jax.nn.relu(h)
            scale = bn_gamma[i] * lax.rsqrt(bn_var[i] + BN_EPS)
            h = h * scale[None, :, None] + (bn_beta[i] - bn_mean[i] * scale)[None, :, None]
            h = h[:, :, :L]
            x = residual + h
        y = _conv1d(x, out_w, 0, 1) + out_b[None, :, None]
        return jnp.transpose(y, (0, 2, 1))

    def _L0_attn_ref(node_features, ln_gamma, ln_beta, W_qkv, W_gate, b_gate, W_final, b_final):
        import jax, jax.numpy as jnp
        import numpy as np
        H, D = (8, 32)
        EPS = 1e-05
        x = node_features
        B, N, _ = x.shape
        mu = jnp.mean(x, axis=-1, keepdims=True)
        var = jnp.mean(jnp.square(x - mu), axis=-1, keepdims=True)
        normed = (x - mu) / jnp.sqrt(var + EPS) * ln_gamma + ln_beta
        qkv = normed @ W_qkv.T
        q, k, v = jnp.split(qkv, 3, axis=-1)

        def to_heads(t):
            return t.reshape(B, N, H, D).transpose(0, 2, 1, 3)
        q, k, v = (to_heads(q), to_heads(k), to_heads(v))
        gate = jax.nn.sigmoid(to_heads(x @ W_gate.T + b_gate))
        scores = jnp.einsum('bhid,bhjd->bhij', q, k) * D ** (-0.5)
        attn = jax.nn.softmax(scores, axis=-1)
        out = jnp.einsum('bhij,bhid->bhjd', attn, v) * gate
        out = out.transpose(0, 2, 1, 3).reshape(B, N, H * D)
        return x + out @ W_final.T + b_final

    def _L0_ffn_ref(x, weight, proj_w, proj_b, scale):
        import jax, jax.numpy as jnp
        import numpy as np
        B, H, E, IN, OUT = (1024, 1, 8, 64, 64)

        @jax.custom_vjp
        def bin_active(x):
            return jnp.sign(x)

        def _ba_fwd(x):
            return (jnp.sign(x), x)

        def _ba_bwd(x, g):
            return (g * (jnp.abs(x) <= 1.0).astype(g.dtype),)
        bin_active.defvjp(_ba_fwd, _ba_bwd)

        @jax.custom_vjp
        def bin_gate(x):
            return (x > 0.5).astype(x.dtype)

        def _bg_fwd(x):
            return ((x > 0.5).astype(x.dtype), None)

        def _bg_bwd(_, g):
            return (g,)
        bin_gate.defvjp(_bg_fwd, _bg_bwd)
        xh = jnp.transpose(x, (1, 0, 2))
        gate = jax.nn.sigmoid(jnp.einsum('hbi,ei->hbe', xh, proj_w) + proj_b)
        gate = bin_gate(gate)
        w = jnp.einsum('hbe,heio->hbio', gate, weight)
        xb = bin_active(xh)
        wb = bin_active(w)
        y = jnp.einsum('hbi,hbio->hbo', xb, wb)
        y = y * scale
        return jnp.transpose(y, (1, 0, 2))
    h = _L0_tok_ref(x, L0_tok_conv_w, L0_tok_conv_b, L0_tok_bn_gamma, L0_tok_bn_beta, L0_tok_bn_mean, L0_tok_bn_var, L0_tok_out_w, L0_tok_out_b)
    h = h + _L0_attn_ref(_layernorm(h, axis=-1), L0_attn_ln_gamma, L0_attn_ln_beta, L0_attn_W_qkv, L0_attn_W_gate, L0_attn_b_gate, L0_attn_W_final, L0_attn_b_final)
    h = h + _L0_ffn_ref(_layernorm(h, axis=-1), L0_ffn_weight, L0_ffn_proj_w, L0_ffn_proj_b, L0_ffn_scale)
    return h

_drawn_inputs = setup_inputs


def setup_inputs(seed=0):
    import zlib

    import numpy as np

    out = dict(_drawn_inputs(seed))
    spreads = {'L0_tok_bn_gamma': (1.0, 0.2),
     'L0_tok_bn_beta': (0.0, 0.1),
     'L0_attn_ln_gamma': (1.0, 0.6),
     'L0_attn_ln_beta': (0.0, 0.8),
     'L0_attn_b_gate': (1.0, 0.6),
     'L0_attn_b_final': (0.0, 0.8)}
    factors = {'L0_tok_out_b': 6.288,
     'L0_attn_W_qkv': 8.0,
     'L0_attn_W_gate': 8.0,
     'L0_attn_W_final': 8.0,
     'L0_ffn_proj_b': 2.794}
    for name, (base, spread) in spreads.items():
        noise = np.random.default_rng([zlib.crc32(name.encode()), seed]).standard_normal(out[name].shape)
        drawn = base * np.exp(spread * noise) if base else spread * noise
        out[name] = jnp.asarray(drawn.astype(out[name].dtype))
    for name, factor in factors.items():
        out[name] = (out[name] * factor).astype(out[name].dtype)
    return out
```

```python
from contextlib import ExitStack

import concourse.bass as bass
from concourse import mybir

F32 = mybir.dt.float32
F16 = mybir.dt.float16
ALU = mybir.AluOpType
ACT = mybir.ActivationFunctionType
AX = mybir.AxisListType

B, CH, N = 16, 4, 375
BLOCKS, TAPS = 9, 3
C = 64
HEADS, D = 8, 32
INNER = HEADS * D
TP, TT = 125, 3
TPAD = TP + 1
HG = 2
E, PATTERNS = 8, 256
PAIRS = C // 2
LOOKS = PAIRS // 2
EPS = 1e-5
SCALE = float(D) ** -0.5
BASE = 256.0
ROUND = 1.5 * 2.0 ** 23
BC = B * CH
CUT = 188
GROUPS = HG * TT
NEG = -1

PLAN = [
    [["tokT", "R3", "look0"], ["q0", "k0", "sum"]],
    [["q1", "k1"], ["final", "look1", "look2"]],
    [["gate0", "look3"], ["gate1", "look4", "v01"]],
    [["v2", "look5", "R0", "look6"], ["sgnT", "look7", "look8"]],
    [["look9", "R1", "look10"], ["logit", "look11", "look12"]],
    [["one0", "look13", "R2"], ["one1", "look14", "look15"]],
]
STAGE = {"tokT": "P", "q0": "P", "q1": "P", "k0": "P", "k1": "P", "gate0": "P", "gate1": "P",
         "v01": "P", "v2": "P", "final": "F", "sgnT": "F", "logit": "F", "one0": "F", "one1": "F",
         "R0": "X", "R1": "X", "R2": "X", "R3": "Y", "sum": "Y"}
STAGE.update({f"look{i}": "X" for i in range(LOOKS)})
FREED_BY_ACT = {"gate0", "gate1", "sgnT", "one0", "one1", "v01", "v2"}


def uses_of(stages):
    return [n for g in PLAN for h in g for n in h if STAGE[n] in stages and n[0] != "R"]


class Ring:

    def __init__(self, stages, used, by_act, by_dve, even, before):
        self.names, self.used, self.by_act, self.by_dve, self.even = uses_of(stages), used, by_act, by_dve, even
        self.before = before

    def bank(self, name):
        return (self.names.index(name) + self.even) % 2

    def filled(self, name):
        return self.used + self.names.index(name) + 1

    def freed(self, name):
        i = self.names.index(name)
        act = name in FREED_BY_ACT
        n = sum((x in FREED_BY_ACT) == act for x in self.names[:i + 1])
        return (self.by_act if act else self.by_dve) + n

    def previous(self, name):
        i = self.names.index(name)
        if i >= 2:
            p = self.names[i - 2]
            return p in FREED_BY_ACT, self.freed(p)
        back = (self.before + self.names)[:2 + i] if len(self.before) == 2 else None
        if back is None:
            hist = self.before + self.names[:i]
            if len(hist) < 2:
                return None
            p = hist[-2]
        else:
            p = back[i]
        act = p in FREED_BY_ACT
        later = self.before[self.before.index(p) + 1:]
        n = sum((x in FREED_BY_ACT) == act for x in later)
        return act, (self.by_act if act else self.by_dve) - n


def build(nc, x, conv_w, conv_p, out_w, ln_g, ln_b, w_in, gate_b, w_fin, fin_b, experts, proj_w, proj_b,
          scale, c_ident, c_sel, c_sum, c_pat, c_score, c_bias, out):
    with ExitStack() as ctx:
        def sb(name, shape, dt=F32):
            return ctx.enter_context(nc.sbuf_tensor(name, shape, dt))

        def psum(name, shape, dt=F32):
            return ctx.enter_context(nc.psum_tensor(name, shape, dt))

        def sem(name):
            return ctx.enter_context(nc.semaphore(name))

        scores = psum("scores", [128, 2, 2, 512])
        attend = psum("attend", [128, 512])
        packed = psum("packed", [128, 512])
        work = psum("work", [128, 2, 512])

        cw = sb("cw", [BC, BLOCKS * TAPS, BC])
        cp = sb("cp", [128, 5, BLOCKS])
        bn_s = sb("bn_s", [BC, BLOCKS])
        bn_t = sb("bn_t", [BC, BLOCKS])
        ow = sb("ow", [BC + 1, B * C])
        lng = sb("lng", [TP, C])
        lnb = sb("lnb", [TP, C])
        finb = sb("finb", [TP, C])
        scl = sb("scl", [TP, C])
        w32 = sb("w32", [128, 4 * INNER])
        wh = sb("wh", [128, 4 * INNER], F16)
        wl = sb("wl", [128, 4 * INNER], F16)
        gb = sb("gb", [128, HG])
        gbh = sb("gbh", [128, HG])
        wf = sb("wf", [128, HG, C])
        wfh = sb("wfh", [128, HG, C])
        ex = sb("ex", [E, 2, PAIRS * C])
        pw32 = sb("pw32", [128, E])
        pwh = sb("pwh", [128, E], F16)
        pwl = sb("pwl", [128, E], F16)
        pb = sb("pb", [E, 1])
        ident = sb("ident", [128, 128], F16)
        sel = sb("sel", [128, LOOKS, PAIRS], F16)
        sums = sb("sums", [128, PAIRS])
        pat = sb("pat", [E, PATTERNS])
        score = sb("score", [E, PATTERNS], F16)
        sbias = sb("sbias", [128, 2])
        half = sb("half", [128, 48])
        xa = [sb(f"xa{i}", [BC + 1, N]) for i in range(2)]
        xt = sb("xt", [BC, N])
        hr = sb("hr", [BC, N])
        H = sb("H", [TP, B, TT, C])
        cen = sb("cen", [TP, B, TT, C])
        sq = sb("sq", [TP, B, TT, C])
        stat = sb("stat", [TP, 6, B, TT])
        sg = sb("sg", [128, 2, 2, PAIRS * C], F16)
        table = sb("table", [128, 2, PAIRS * C], F16)
        zn = sb("zn", [TP, 2, TT, C])
        tmp = sb("tmp", [TP, TT, C])
        zsp = [sb(f"zsp{i}", [TP, 2, TT, 2, C], F16) for i in range(2)]
        znT = sb("znT", [128, 2, N], F16)
        qk = sb("qk", [128, 4, HG, N], F16)
        stack = [sb(f"stack{i}", [128, 2, 4, HG, N], F16) for i in range(2)]
        vv = [sb(f"vv{i}", [TP, TT, INNER]) for i in range(2)]
        gate = [sb(f"gate{i}", [128, HG, N]) for i in range(2)]
        mx = sb("mx", [TP, 2, 4])
        probs = sb("probs", [TP, 2, 4, N])
        rs = sb("rs", [TP, 2, 4])
        ri = sb("ri", [TP, 2, 4])
        vn = sb("vn", [TP, 2, 4, D])
        att = sb("att", [128, HG, N])
        x3 = [sb(f"x3_{i}", [TP, TT, C]) for i in range(2)]
        c3 = sb("c3", [TP, TT, C])
        q3 = sb("q3", [TP, TT, C])
        z3 = sb("z3", [TP, TT, C])
        st3 = sb("st3", [TP, 4, TT])
        zsg = sb("zsg", [TP, 2, TT, 2, C], F16)
        zxT = [sb(f"zxT{i}", [128, 2, N], F16) for i in range(2)]
        bits = sb("bits", [E, N], F16)
        onehot = [sb(f"onehot{i}", [128, 2, N], F16) for i in range(2)]
        prod = sb("prod", [128, 8, N], F16)
        pk = sb("pk", [128, N])
        dig = sb("dig", [TP, TT, PAIRS])
        yy = sb("yy", [TP, TT, PAIRS, 2])
        yo = sb("yo", [TP, TT, C])

        ld_conv, ld_x, ld_ow, ld_ex, ld_w, ld_c = (sem(n) for n in ("ld_conv", "ld_x", "ld_ow", "ld_ex", "ld_w", "ld_c"))
        consts_set = sem("consts_set")
        ones_set = sem("ones_set")
        bn_ready = sem("bn_ready")
        conv_done = sem("conv_done")
        relu_lo, relu_hi = sem("relu_lo"), sem("relu_hi")
        shifted = sem("shifted")
        x_ready = sem("x_ready")
        h_done = sem("h_done")
        h_copied_v, h_copied_a = sem("h_copied_v"), sem("h_copied_a")
        tab_done, sg_ready = sem("tab_done"), sem("sg_ready")
        tab_ready = sem("tab_ready")
        w_pool, w_act, w_ready = sem("wp"), sem("wa"), sem("w_ready")
        ln_v, ln_a, ln_p = sem("ln_v"), sem("ln_a"), sem("ln_p")
        work_full, work_act, work_dve = sem("work_full"), sem("work_act"), sem("work_dve")
        zn_ready, pool_link, dve_link = sem("zn_ready"), sem("pool_link"), sem("dve_link")
        high_ready, stacked = sem("high_ready"), sem("stacked")
        scored, max_ready, exp_done = sem("scored"), sem("max_ready"), sem("exp_done")
        sum_inverse, v_ready, av_done, gated = sem("sum_inverse"), sem("v_ready"), sem("av_done"), sem("gated")
        cen_ready, sq_ready, var_ready, split_ready, sign_ready = (
            sem("cen_ready"), sem("sq_ready"), sem("var_ready"), sem("split_ready"), sem("sign_ready"))
        bits_ready = sem("bits_ready")
        cen_sum, norm_link, out_link = sem("cen_sum"), sem("norm_link"), sem("out_link")
        reduced, pk_copied, digits, y_ready, stored = (
            sem("reduced"), sem("pk_copied"), sem("digits"), sem("y_ready"), sem("stored"))

        block = ctx.enter_context(nc.Block())

        STEPS = B + 3
        LOOP0, LOOP1 = 4, 14

        def stages(s):
            on = {"P": 0 <= s + 1 < B, "F": 0 <= s - 1 < B, "X": 0 <= s - 2 < B, "Y": 0 <= s - 3 < B}
            return "".join(k for k in on if on[k])

        full = uses_of("PFXY")
        per_act = sum(n in FREED_BY_ACT for n in full)
        per_dve = len(full) - per_act

        def run_steps(eng, step):
            used = by_act = by_dve = 0
            before = []
            s = -1
            while s < STEPS:
                st = stages(s)
                names = uses_of(st)
                if s == LOOP0:
                    turns = (LOOP1 - LOOP0) // 2
                    with eng.Fori(0, turns) as j:
                        for k in range(2):
                            ring = Ring(st, j * (2 * len(full)) + (used + k * len(full)),
                                        j * (2 * per_act) + (by_act + k * per_act),
                                        j * (2 * per_dve) + (by_dve + k * per_dve),
                                        (used + k * len(full)) % 2, before[-2:] if k == 0 else names[-2:])
                            step(j * 2 + (s + k), (s + k) % 2, st + "A", ring)
                    used, by_act, by_dve = (used + 2 * turns * len(full), by_act + 2 * turns * per_act,
                                            by_dve + 2 * turns * per_dve)
                    s = LOOP1
                else:
                    step(s, s % 2, st + ("A" if 0 <= s < B else ""),
                         Ring(st, used, by_act, by_dve, used % 2, before[-2:]))
                    used += len(names)
                    by_act += sum(n in FREED_BY_ACT for n in names)
                    by_dve += sum(n not in FREED_BY_ACT for n in names)
                    s += 1
                before = before + names

        def transposed_tiles(bank):
            return work[:, bank, :].bitcast(F16)[:, 0:2 * TT * TPAD].rearrange("p (i n) -> p i n", n=TPAD)[:, :, 0:TP]

        def geq(eng, semaphore, count):
            if not isinstance(count, int) or count > 0:
                eng.wait_ge(semaphore, count)

        @block.sync
        def _(sp):
            sp.dma_start(xa[0][0:BC, :], x).then_inc(ld_x, 16)
            sp.dma_start(cw[:], conv_w).then_inc(ld_conv, 16)
            sp.dma_start(cp[:], conv_p).then_inc(ld_conv, 16)
            sp.dma_start(pat[:], c_pat).then_inc(ld_ex, 16)
            sp.dma_start(ex[:], experts).then_inc(ld_ex, 16)
            sp.dma_start(ow[:], out_w).then_inc(ld_ow, 16)
            for r in range(2):
                sp.dma_start(w32[C * r:C * r + C, :], w_in).then_inc(ld_w, 16)
                sp.dma_start(pw32[C * r:C * r + C, :], proj_w).then_inc(ld_w, 16)
            sp.dma_start(wf[:], w_fin).then_inc(ld_w, 16)
            sp.dma_start(gb[:], gate_b).then_inc(ld_w, 16)
            for dst, src in ((ident, c_ident), (sel, c_sel), (sums, c_sum), (score, c_score), (sbias, c_bias),
                             (pb, proj_b)):
                sp.dma_start(dst[:], src).then_inc(ld_c, 16)
            for dst, src in ((lng, ln_g), (lnb, ln_b), (finb, fin_b), (scl, scale)):
                sp.dma_start(dst[:], src.partition_broadcast(TP)).then_inc(ld_c, 16)

            def step(s, par, st, ring):
                if "Y" in st:
                    dst = out[s - 3:s - 2] if isinstance(s, int) else out[bass.ds(sp.snap(s - 3), 1)]
                    sp.wait_ge(y_ready, s - 3 + 1)
                    sp.dma_start(dst.rearrange("o (p t) c -> (o p) t c", t=TT), yo[:]).then_inc(stored, 16)
                if "P" in st:
                    b = s + 1
                    sp.wait_ge(work_dve, ring.freed("k1"))
                    geq(sp, stacked, 256 * b)
                    for r in range(4):
                        qi, ki = r // 2, 2 + r % 2
                        for h in range(4):
                            sp.dma_start(stack[1 - par][D * r:D * r + D, :, h, :, :],
                                         qk[D * h:D * h + D, qi:ki + 1:ki - qi, :, :]).then_inc(stacked, 16)

            run_steps(sp, step)
            sp.wait_ge(stored, 16 * B)

        @block.tensor
        def _(pe):
            def table_mm(i):
                bank = (attend, packed)[i % 2]
                if i == 0:
                    pe.wait_ge(ld_ex, 32)
                if i >= 2:
                    pe.wait_ge(sg_ready, i - 1)
                hp, dg, ch = i // 8, i // 4 % 2, i % 4
                pe.matmul(bank[:], pat[:, 128 * hp:128 * hp + 128], ex[:, dg, 512 * ch:512 * ch + 512],
                          start=True, stop=True).then_inc(tab_done, 1)

            pe.wait_ge(ld_conv, 32)
            pe.wait_ge(ld_x, 16)
            for n in range(BLOCKS):
                d = 2 ** n
                geq(pe, x_ready, n)
                cur = xa[n % 2]
                cuts = ((0, CUT), (CUT, N))
                spans = [[(k, max(lo, (2 - k) * d), hi) for k in (2, 1, 0) if max(lo, (2 - k) * d) < hi] for lo, hi in cuts]
                for t in range(TAPS):
                    for c in range(2):
                        if t >= len(spans[c]):
                            continue
                        k, lo, hi = spans[c][t]
                        sh = (2 - k) * d
                        mm = pe.matmul(scores[BC * c:BC * c + BC, n % 2, 0, lo - cuts[c][0]:hi - cuts[c][0]],
                                       cw[:, n * TAPS + k, :], cur[0:BC, lo - sh:hi - sh],
                                       start=(t == 0), stop=(t == len(spans[c]) - 1), skip_group_check=True)
                mm.then_inc(conv_done, 1)
                table_mm(n)
            pe.wait_ge(x_ready, BLOCKS)
            pe.wait_ge(ones_set, 2)
            pe.wait_ge(ld_ow, 16)
            for i in range(2 * TT):
                t, bh = i // 2, i % 2
                if i >= 4:
                    pe.wait_ge((h_copied_v, h_copied_a)[i % 2], (i - 4) // 2 + 1)
                pe.matmul(scores[0:TP, i % 4 // 2, i % 2, :], xa[BLOCKS % 2][:, t:N:TT], ow[:, 512 * bh:512 * bh + 512],
                          start=True, stop=True).then_inc(h_done, 1)
            for i in range(BLOCKS, 16):
                table_mm(i)
            pe.wait_ge(w_ready, 1)
            pe.wait_ge(ld_c, 160)
            pe.wait_ge(sg_ready, 16)
            pe.wait_ge(h_copied_v, TT)
            pe.wait_ge(h_copied_a, TT)

            def step(s, par, st, ring):
                nxt = 1 - par

                def open_bank(name):
                    prev = ring.previous(name)
                    if prev:
                        pe.wait_ge(work_act if prev[0] else work_dve, prev[1])
                    return work[:, ring.bank(name), :]

                def tokT():
                    pe.wait_ge(zn_ready, s + 2)
                    o = open_bank("tokT").bitcast(F16)
                    for i in range(2):
                        for t in range(TT):
                            mm = pe.transpose(o[:, TPAD * (TT * i + t):TPAD * (TT * i + t) + TP],
                                              zsp[nxt][:, i, t, :, :].rearrange("p a c -> p (a c)"), ident[0:TP, 0:TP])
                    mm.then_inc(work_full, 1)

                def feature_major(name, col, src):
                    if name == "q0":
                        pe.wait_ge(work_dve, ring.freed("tokT"))
                    o = open_bank(name)
                    pe.matmul(o[:, 0:N], wh[:, col:col + 128], znT[:, src, :], start=True, stop=False)
                    pe.matmul(o[:, 0:N], wl[:, col:col + 128], znT[:, src, :], start=False, stop=True).then_inc(work_full, 1)

                def token_major(name, tiles):
                    o = open_bank(name)
                    for j, t in enumerate(tiles):
                        for w in (wh, wl):
                            mm = pe.matmul(o[0:TP, INNER * j:INNER * j + INNER], znT[:, 1, TP * t:TP * t + TP],
                                           w[:, 2 * INNER:3 * INNER], start=(w is wh), stop=(w is wl))
                    mm.then_inc(work_full, 1)

                def final():
                    pe.wait_ge(gated, 2 * (s - 1) + 2)
                    o = open_bank("final")
                    for t in range(TT):
                        for g in range(HG):
                            mm = pe.matmul(o[0:TP, C * t:C * t + C], att[:, g, TP * t:TP * t + TP], wfh[:, g, :],
                                           start=(g == 0), stop=(g == HG - 1))
                    mm.then_inc(work_full, 1)

                def sgnT():
                    pe.wait_ge(split_ready, s)
                    pe.wait_ge(sign_ready, s)
                    o = open_bank("sgnT").bitcast(F16)
                    for i in range(2):
                        for t in range(TT):
                            mm = pe.transpose(o[:, TPAD * (TT * i + t):TPAD * (TT * i + t) + TP],
                                              zsg[:, i, t, :, :].rearrange("p a c -> p (a c)"), ident[0:TP, 0:TP])
                    mm.then_inc(work_full, 1)

                def logit():
                    pe.wait_ge(work_act, ring.freed("sgnT"))
                    o = open_bank("logit")
                    pe.matmul(o[0:E, 0:N], pwh[:], zxT[nxt][:, 0, :], start=True, stop=False)
                    pe.matmul(o[0:E, 0:N], pwl[:], zxT[nxt][:, 0, :], start=False, stop=True).then_inc(work_full, 1)

                def one(i):
                    if i == 0:
                        pe.wait_ge(work_dve, ring.freed("logit"))
                    o = open_bank(f"one{i}")
                    pe.matmul(o[:, 0:N], score[:, 128 * i:128 * i + 128], bits[:], start=True,
                              stop=True).then_inc(work_full, 1)

                def look(r):
                    o = open_bank(f"look{r}")
                    pe.matmul(o[:, 0:N], table[:, 0, 128 * r:128 * r + 128], onehot[par][:, 0, :], start=True, stop=False)
                    pe.matmul(o[:, 0:N], table[:, 1, 128 * r:128 * r + 128], onehot[par][:, 1, :], start=False,
                              stop=True).then_inc(work_full, 1)

                def reduce(q, b):
                    if q == 0:
                        geq(pe, pk_copied, b)
                    if q < 3:
                        pe.wait_ge(work_dve, ring.freed(f"look{4 * q + 3}"))
                    for c in range(4):
                        r = 4 * q + c
                        mm = pe.matmul(packed[32 * c:32 * c + 32, 0:N], sel[:, r, :], prod[:, r % 8, :],
                                       start=(q == 0), stop=(q == 3), skip_group_check=True)
                    mm.then_inc(reduced, 1)

                def total():
                    pe.wait_ge(pk_copied, s - 2)
                    o = open_bank("sum")
                    for t in range(TT):
                        mm = pe.matmul(o[0:TP, PAIRS * t:PAIRS * t + PAIRS], pk[:, TP * t:TP * t + TP], sums[:],
                                       start=True, stop=True)
                    mm.then_inc(work_full, 1)

                def last_reduce():
                    pe.wait_ge(work_dve, ring.by_dve)
                    reduce(3, s - 3)

                def sum_queries(b, g, slot):
                    pe.wait_ge(v_ready, 6 * b + g + 1)
                    if g % TT == 0:
                        geq(pe, gated, 2 * b + g // TT)
                    for h in range(4):
                        mm = pe.matmul(attend[32 * h:32 * h + 32, 0:N], vn[:, slot, h, :], probs[:, slot, h, :],
                                       start=(g % TT == 0), stop=(g % TT == TT - 1), skip_group_check=True)
                    mm.then_inc(av_done, 1)

                todo = {"tokT": tokT, "q0": lambda: feature_major("q0", 0, 1), "q1": lambda: feature_major("q1", 128, 1),
                        "k0": lambda: feature_major("k0", INNER, 1), "k1": lambda: feature_major("k1", INNER + 128, 1),
                        "gate0": lambda: feature_major("gate0", 3 * INNER, 0),
                        "gate1": lambda: feature_major("gate1", 3 * INNER + 128, 0),
                        "v01": lambda: token_major("v01", (0, 1)), "v2": lambda: token_major("v2", (2,)),
                        "final": final, "sgnT": sgnT, "logit": logit, "one0": lambda: one(0), "one1": lambda: one(1),
                        "R0": lambda: reduce(0, s - 2), "R1": lambda: reduce(1, s - 2), "R2": lambda: reduce(2, s - 2),
                        "R3": last_reduce, "sum": total}
                for r in range(LOOKS):
                    todo[f"look{r}"] = lambda r=r: look(r)
                if "A" in st:
                    pe.wait_ge(stacked, 256 * (s + 1))
                for g in range(GROUPS):
                    hg, t = g // TT, g % TT
                    for p in range(2):
                        if "A" in st:
                            geq(pe, exp_done, 24 * s + 4 * (g - 1) + 2 * p + 2)
                            for h in range(2):
                                mm = pe.matmul(scores[0:TP, p, h, 0:N], stack[par][:, 0, 2 * p + h, hg, TP * t:TP * t + TP],
                                               stack[par][:, 1, 2 * p + h, hg, :], start=True, stop=True)
                            mm.then_inc(scored, 1)
                        for name in PLAN[g][p]:
                            if STAGE[name] in st:
                                todo[name]()
                        if p == 1:
                            if g == 0 and "F" in st:
                                sum_queries(s - 1, 5, 1)
                            if g > 0 and "A" in st:
                                sum_queries(s, g - 1, (g - 1) % 2)

            run_steps(pe, step)

        @block.scalar
        def _(act):
            def table_sign(i):
                act.wait_ge(tab_done, i + 1)
                hp, dg, ch = i // 8, i // 4 % 2, i % 4
                act.activation(sg[:, hp, dg, 512 * ch:512 * ch + 512], (attend, packed)[i % 2][:],
                               ACT.Sign).then_inc(sg_ready, 1)

            act.wait_ge(ld_conv, 32)
            for n in range(BLOCKS):
                act.wait_ge(conv_done, n + 1)
                act.activation(hr[:, CUT:N], scores[BC:2 * BC, n % 2, 0, 0:N - CUT], ACT.Relu,
                               bias=cp[BC:2 * BC, 0, n:n + 1]).then_inc(relu_hi, 1)
                table_sign(n)
            for i in range(1, 2 * TT, 2):
                t, bh = i // 2, i % 2
                act.wait_ge(h_done, i + 1)
                act.activation(H[:, 8 * bh:8 * bh + 8, t, :], scores[0:TP, i % 4 // 2, 1, :].rearrange("p (b c) -> p b c", c=C),
                               ACT.Copy).then_inc(h_copied_a, 1)
            act.wait_ge(ld_w, 96)
            act.activation(wh[:], w32[:], ACT.Copy).then_inc(w_act, 1)
            for i in range(BLOCKS, 16):
                table_sign(i)
            act.wait_ge(ln_v, 2)
            act.activation(sq[:].rearrange("p b t c -> p (b t c)"), cen[:].rearrange("p b t c -> p (b t c)"),
                           ACT.Square).then_inc(ln_a, 1)

            def step(s, par, st, ring):
                nxt = 1 - par

                def high(i):
                    name = ("q0", "q1", "k0", "k1")[i]
                    if name == "q0":
                        geq(act, stacked, 256 * (s + 1))
                    act.wait_ge(work_full, ring.filled(name))
                    act.activation(qk[:, 2 * (i // 2), i % 2, :], work[:, ring.bank(name), 0:N], ACT.Copy,
                                   scale=(-SCALE if i < 2 else 1.0)).then_inc(high_ready, 1)

                def gates(i):
                    name = f"gate{i}"
                    if i == 0:
                        geq(act, gated, 2 * s)
                    act.wait_ge(work_full, ring.filled(name))
                    act.activation(gate[nxt][:, i, :], work[:, ring.bank(name), 0:N], ACT.Tanh, bias=gbh[:, i:i + 1],
                                   scale=0.5).then_inc(work_act, 1)

                def values(name, t, n):
                    if name == "v01":
                        geq(act, v_ready, 6 * s)
                    act.wait_ge(work_full, ring.filled(name))
                    act.activation(vv[nxt][:, t:t + n, :].rearrange("p t c -> p (t c)"),
                                   work[0:TP, ring.bank(name), 0:INNER * n], ACT.Copy).then_inc(work_act, 1)

                def sign():
                    act.wait_ge(cen_ready, s)
                    for r in range(2):
                        a = act.activation(zsg[:, 1, :, r, :], c3[:], ACT.Sign)
                    a.then_inc(sign_ready, 1)

                def transposed():
                    act.wait_ge(work_full, ring.filled("sgnT"))
                    act.activation(zxT[nxt][:].rearrange("p a (t n) -> p (a t) n", t=TT),
                                   transposed_tiles(ring.bank("sgnT")), ACT.Copy).then_inc(work_act, 1)

                def one(i):
                    name = f"one{i}"
                    act.wait_ge(work_full, ring.filled(name))
                    act.activation(onehot[nxt][:, i, :], work[:, ring.bank(name), 0:N], ACT.Relu,
                                   bias=sbias[:, i:i + 1]).then_inc(work_act, 1)

                def copy_packed():
                    act.wait_ge(reduced, 4 * (s - 3) + 4)
                    act.activation(pk[:], packed[:, 0:N], ACT.Copy).then_inc(pk_copied, 1)

                todo = {"q0": lambda: high(0), "q1": lambda: high(1), "k0": lambda: high(2), "k1": lambda: high(3),
                        "gate0": lambda: gates(0), "gate1": lambda: gates(1), "v01": lambda: values("v01", 0, 2),
                        "v2": lambda: values("v2", 2, 1), "sgnT": transposed, "one0": lambda: one(0),
                        "one1": lambda: one(1), "R3": copy_packed}
                for g in range(GROUPS):
                    for p in range(2):
                        if "A" in st:
                            act.wait_ge(max_ready, 12 * s + 2 * g + p + 1)
                            if p == 0:
                                geq(act, av_done, 6 * s + g - 1)
                            for h in range(2):
                                i = 2 * p + h
                                act.activation(probs[:, g % 2, i, :], scores[0:TP, p, h, 0:N], ACT.Exp, scale=-1.0,
                                               bias=mx[:, g % 2, i:i + 1],
                                               accum_out=rs[:, g % 2, i:i + 1]).then_inc(exp_done, 1)
                        for name in PLAN[g][p]:
                            if STAGE[name] in st and name in todo:
                                todo[name]()
                        if g == 2 and p == 0 and "F" in st:
                            sign()

            run_steps(act, step)

        @block.vector
        def _(dve):
            link = [0]

            def then(ins):
                link[0] += 1
                ins.then_inc(dve_link, 1)
                dve.wait_ge(dve_link, link[0])

            for i in range(2):
                dve.memset(xa[i][BC:BC + 1, :], 1.0).then_inc(ones_set, 1)
            dve.wait_ge(ld_conv, 32)
            for n in range(BLOCKS):
                cur, new = xa[n % 2], xa[(n + 1) % 2]
                dve.wait_ge(conv_done, n + 1)
                dve.tensor_scalar(hr[:, 0:CUT], scores[0:BC, n % 2, 0, 0:CUT], cp[0:BC, 0, n:n + 1], 0.0,
                                  ALU.add, ALU.max).then_inc(relu_lo, 1)
                dve.wait_ge(relu_lo, n + 1)
                dve.wait_ge(relu_hi, n + 1)
                dve.wait_ge(shifted, n + 1)
                dve.scalar_tensor_tensor(new[0:BC, :], hr[:], bn_s[:, n:n + 1], xt[:], ALU.mult, ALU.add).then_inc(x_ready, 1)
            for i in range(0, 2 * TT, 2):
                t, bh = i // 2, i % 2
                dve.wait_ge(h_done, i + 1)
                dve.tensor_copy(H[:, 8 * bh:8 * bh + 8, t, :],
                                scores[0:TP, i % 4 // 2, 0, :].rearrange("p (b c) -> p b c", c=C)).then_inc(h_copied_v, 1)
            dve.wait_ge(h_copied_v, TT)
            dve.wait_ge(h_copied_a, TT)
            s1, v1, m1 = stat[:, 0], stat[:, 1], stat[:, 4]
            dve.tensor_reduce(s1, H[:], AX.X, ALU.add).then_inc(ln_v, 1)
            dve.wait_ge(ln_v, 1)
            dve.scalar_tensor_tensor(cen[:].rearrange("p b t c -> p (b t) c"),
                                     s1.rearrange("p b t -> p (b t)").unsqueeze(2).to_broadcast([TP, B * TT, C]), -1.0 / C,
                                     H[:].rearrange("p b t c -> p (b t) c"), ALU.mult, ALU.add).then_inc(ln_v, 1)
            dve.wait_ge(w_act, 1)
            dve.tensor_tensor(wl[:], w32[:], wh[:], ALU.subtract)
            then(dve.tensor_copy(pwh[:], pw32[:]))
            dve.tensor_tensor(pwl[:], pw32[:], pwh[:], ALU.subtract)
            dve.tensor_scalar(gbh[:], gb[:], 0.5, None, ALU.mult)
            dve.tensor_scalar(wfh[:], wf[:], 0.5, None, ALU.mult).then_inc(w_ready, 1)
            dve.wait_ge(ln_a, 1)
            dve.tensor_reduce(v1, sq[:], AX.X, ALU.add).then_inc(ln_v, 1)
            dve.wait_ge(sg_ready, 16)
            dve.scalar_tensor_tensor(table[:], sg[:, :, 1, :], BASE, sg[:, :, 0, :], ALU.mult, ALU.add).then_inc(tab_ready, 1)
            dve.wait_ge(ld_c, 160)

            def step(s, par, st, ring):
                nxt = 1 - par

                def tokT():
                    dve.wait_ge(work_full, ring.filled("tokT"))
                    dve.tensor_copy(znT[:].rearrange("p a (t n) -> p (a t) n", t=TT),
                                    transposed_tiles(ring.bank("tokT"))).then_inc(work_dve, 1)

                def low(i):
                    name = ("q0", "q1", "k0", "k1")[i]
                    dve.wait_ge(high_ready, 4 * (s + 1) + (1, 3, 2, 4)[i])
                    dve.scalar_tensor_tensor(qk[:, 2 * (i // 2) + 1, i % 2, :], work[:, ring.bank(name), 0:N],
                                             (-SCALE if i < 2 else 1.0), qk[:, 2 * (i // 2), i % 2, :], ALU.mult,
                                             ALU.subtract).then_inc(work_dve, 1)

                def final():
                    dve.wait_ge(work_full, ring.filled("final"))
                    if "Y" in st or "X" in st:
                        geq(dve, y_ready, s - 2)
                    hz = H[:, bass.ds(s - 1, 1)] if not isinstance(s, int) else H[:, s - 1:s]
                    xr = x3[nxt][:].rearrange("p t c -> p (t c)")
                    dve.tensor_tensor(xr, work[0:TP, ring.bank("final"), 0:TT * C],
                                      hz.rearrange("p o t c -> p (o t c)"), ALU.add).then_inc(work_dve, 1)
                    dve.wait_ge(work_dve, ring.freed("final"))
                    dve.tensor_reduce(st3[:, 0], x3[nxt][:], AX.X, ALU.add).then_inc(cen_sum, 1)
                    dve.wait_ge(cen_sum, s)
                    dve.scalar_tensor_tensor(c3[:], st3[:, 0].unsqueeze(2).to_broadcast([TP, TT, C]), -1.0 / C, x3[nxt][:],
                                             ALU.mult, ALU.add).then_inc(cen_ready, 1)

                def variance():
                    dve.wait_ge(sq_ready, s)
                    dve.tensor_reduce(st3[:, 1], q3[:], AX.X, ALU.add).then_inc(var_ready, 1)
                    dve.wait_ge(var_ready, 2 * (s - 1) + 1)
                    dve.tensor_scalar(st3[:, 2], st3[:, 1], 1.0 / C, EPS, ALU.mult, ALU.add).then_inc(var_ready, 1)

                def logit():
                    dve.wait_ge(work_full, ring.filled("logit"))
                    dve.tensor_scalar(bits[:], work[0:E, ring.bank("logit"), 0:N], pb[:], 0.0, ALU.add,
                                      ALU.is_gt).then_inc(work_dve, 1)

                def look(r):
                    name = f"look{r}"
                    dve.wait_ge(work_full, ring.filled(name))
                    if r % 4 == 0:
                        geq(dve, reduced, 4 * (s - 2) + r // 4 - 1)
                    dve.tensor_tensor(prod[:, r % 8, :], work[:, ring.bank(name), 0:N], zxT[par][:, 1, :],
                                      ALU.mult).then_inc(work_dve, 1)

                def unpack():
                    dve.wait_ge(work_full, ring.filled("sum"))
                    geq(dve, y_ready, s - 3)
                    o = work[0:TP, ring.bank("sum"), 0:TT * PAIRS].rearrange("p (t c) -> p t c", t=TT)
                    dve.tensor_scalar(dig[:], o, 1.0 / BASE, ROUND, ALU.mult, ALU.add).then_inc(digits, 1)
                    dve.wait_ge(digits, 2 * (s - 3) + 1)
                    dve.tensor_scalar(yy[:, :, :, 1], dig[:], -ROUND, None, ALU.add).then_inc(digits, 1)
                    dve.wait_ge(digits, 2 * (s - 3) + 2)
                    dve.scalar_tensor_tensor(yy[:, :, :, 0], yy[:, :, :, 1], -BASE, o, ALU.mult, ALU.add).then_inc(work_dve, 1)

                todo = {"tokT": tokT, "q0": lambda: low(0), "q1": lambda: low(1), "k0": lambda: low(2),
                        "k1": lambda: low(3), "final": final, "logit": logit, "sum": unpack}
                for r in range(LOOKS):
                    todo[f"look{r}"] = lambda r=r: look(r)

                def inverse(b, slot, g):
                    dve.wait_ge(exp_done, 24 * b + 4 * g + 4)
                    dve.reciprocal(ri[:, slot, :], rs[:, slot, :]).then_inc(sum_inverse, 1)

                def apply_gate(b, hg, which):
                    dve.wait_ge(av_done, 6 * b + TT * hg + TT)
                    dve.scalar_tensor_tensor(att[:, hg, :], gate[which][:, hg, :], 1.0, attend[:, 0:N], ALU.add,
                                             ALU.mult).then_inc(gated, 1)

                for g in range(GROUPS):
                    for p in range(2):
                        if "A" in st:
                            dve.wait_ge(scored, 12 * s + 2 * g + p + 1)
                            dve.tensor_reduce(mx[:, g % 2, 2 * p:2 * p + 2], scores[0:TP, p, :, 0:N], AX.X,
                                              ALU.min).then_inc(max_ready, 1)
                        if p == 0:
                            if g == 0 and "F" in st:
                                inverse(s - 1, 1, 5)
                            if g > 0 and "A" in st:
                                inverse(s, (g - 1) % 2, g - 1)
                        for name in PLAN[g][p]:
                            if STAGE[name] in st and name in todo:
                                todo[name]()
                        if g == 0 and p == 1 and "F" in st:
                            apply_gate(s - 1, 1, nxt)
                        if g == 3 and p == 1 and "A" in st:
                            apply_gate(s, 0, par)
                        if g == 2 and p == 0 and "F" in st:
                            variance()

            run_steps(dve, step)

        @block.gpsimd
        def _(pool):
            link = [0]

            pool.memset(half[:], -0.5).then_inc(consts_set, 1)
            pool.wait_ge(consts_set, 1)
            pool.wait_ge(ld_conv, 32)
            pool.tensor_scalar(bn_s[:], cp[0:BC, 4, :], EPS, None, ALU.add).then_inc(bn_ready, 1)
            pool.wait_ge(bn_ready, 1)
            pool.tensor_tensor(bn_t[:], bn_s[:], half[0:BC, 0:BLOCKS], ALU.pow).then_inc(bn_ready, 1)
            pool.wait_ge(bn_ready, 2)
            pool.tensor_tensor(bn_s[:], bn_t[:], cp[0:BC, 1, :], ALU.mult).then_inc(bn_ready, 1)
            pool.wait_ge(bn_ready, 3)
            pool.tensor_tensor(bn_t[:], bn_s[:], cp[0:BC, 3, :], ALU.mult).then_inc(bn_ready, 1)
            pool.wait_ge(bn_ready, 4)
            pool.tensor_tensor(bn_t[:], cp[0:BC, 2, :], bn_t[:], ALU.subtract).then_inc(bn_ready, 1)
            pool.wait_ge(bn_ready, 5)
            pool.wait_ge(ld_x, 16)
            for n in range(BLOCKS):
                geq(pool, x_ready, n)
                pool.tensor_scalar(xt[:], xa[n % 2][0:BC, :], bn_t[:, n:n + 1], None, ALU.add).then_inc(shifted, 1)
            s1, v1, r1, r2, t1, t2 = (stat[:, i] for i in range(6))
            hv = half[0:TP, :].rearrange("p (b t) -> p b t", t=TT)

            def chain(ins):
                link[0] += 1
                ins.then_inc(ln_p, 1)
                pool.wait_ge(ln_p, link[0])

            pool.wait_ge(ln_v, 3)
            chain(pool.tensor_scalar(t1, v1, 1.0 / C, EPS, ALU.mult, ALU.add))
            chain(pool.tensor_tensor(r1, t1, hv, ALU.pow))
            chain(pool.tensor_tensor(t2, r1, r1, ALU.mult))
            chain(pool.tensor_tensor(t1, t2, v1, ALU.mult))
            chain(pool.tensor_scalar(t2, t1, 1.0 / C, EPS, ALU.mult, ALU.add))
            chain(pool.tensor_tensor(r2, t2, hv, ALU.pow))
            pool.wait_ge(ld_c, 160)

            def normalise(b, par):
                def one_b(a):
                    return a[:, bass.ds(b, 1)] if not isinstance(b, int) else a[:, b:b + 1]

                def wide(v):
                    return v.rearrange("p o t -> p (o t)").unsqueeze(2).to_broadcast([TP, TT, C])

                def rows(v):
                    return v[:].unsqueeze(1).to_broadcast([TP, TT, C])

                zt, nt = zn[:, 0], zn[:, 1]
                high = [zsp[par][:, i, :, 0, :] for i in range(2)]
                low = [zsp[par][:, i, :, 1, :] for i in range(2)]
                hb = one_b(H).rearrange("p o t c -> p (o t) c")
                k = 9 * b
                geq(pool, pool_link, k)
                geq(pool, zn_ready, b)

                def nxt(ins, i):
                    ins.then_inc(pool_link, 1)
                    pool.wait_ge(pool_link, k + i)

                cb, r1b = one_b(cen).rearrange("p o t c -> p (o t) c"), wide(one_b(stat[:, 2]))
                pool.tensor_tensor(high[0], cb, r1b, ALU.mult).then_inc(pool_link, 1)
                nxt(pool.tensor_tensor(zt, cb, r1b, ALU.mult), 2)
                nxt(pool.tensor_tensor(tmp[:], zt, wide(one_b(stat[:, 3])), ALU.mult), 3)
                nxt(pool.tensor_tensor(nt, tmp[:], rows(lng), ALU.mult), 4)
                pool.tensor_tensor(high[1], nt, rows(lnb), ALU.add).then_inc(pool_link, 1)
                pool.tensor_tensor(tmp[:], zt, rows(finb), ALU.add).then_inc(pool_link, 1)
                nxt(pool.tensor_tensor(nt, nt, rows(lnb), ALU.add), 7)
                pool.tensor_tensor(hb, hb, tmp[:], ALU.add).then_inc(pool_link, 1)
                pool.tensor_tensor(low[0], zt, high[0], ALU.subtract).then_inc(pool_link, 1)
                pool.tensor_tensor(low[1], nt, high[1], ALU.subtract).then_inc(zn_ready, 1)

            normalise(0, 0)

            def step(s, par, st, ring):
                nxt = 1 - par

                def scale_values(b, g, slot, which):
                    pool.wait_ge(sum_inverse, 6 * b + g + 1)
                    geq(pool, av_done, 6 * b + g - 1)
                    hg, t = g // TT, g % TT
                    pool.tensor_tensor(vn[:, slot], vv[which][:, t, 128 * hg:128 * hg + 128].rearrange("p (h d) -> p h d", d=D),
                                       ri[:, slot, :].unsqueeze(2).to_broadcast([TP, 4, D]), ALU.mult).then_inc(v_ready, 1)

                def square():
                    pool.wait_ge(cen_ready, s)
                    pool.tensor_tensor(q3[:], c3[:], c3[:], ALU.mult).then_inc(sq_ready, 1)

                def norm3():
                    k = 3 * (s - 1)
                    pool.wait_ge(var_ready, 2 * s)
                    geq(pool, split_ready, s - 1)
                    pool.tensor_tensor(st3[:, 3], st3[:, 2], half[0:TP, 0:TT], ALU.pow).then_inc(norm_link, 1)
                    pool.wait_ge(norm_link, k + 1)
                    wide = st3[:, 3].unsqueeze(2).to_broadcast([TP, TT, C])
                    pool.tensor_tensor(zsg[:, 0, :, 0, :], c3[:], wide, ALU.mult).then_inc(norm_link, 1)
                    pool.tensor_tensor(z3[:], c3[:], wide, ALU.mult).then_inc(norm_link, 1)
                    pool.wait_ge(norm_link, k + 3)
                    pool.tensor_tensor(zsg[:, 0, :, 1, :], z3[:], zsg[:, 0, :, 0, :], ALU.subtract).then_inc(split_ready, 1)

                def output():
                    pool.wait_ge(work_dve, ring.freed("sum"))
                    geq(pool, stored, 16 * (s - 3))
                    y3 = yy[:].rearrange("p t c g -> p t (c g)")
                    pool.tensor_tensor(yo[:], y3, scl[:].unsqueeze(1).to_broadcast([TP, TT, C]), ALU.mult).then_inc(out_link, 1)
                    pool.wait_ge(out_link, s - 2)
                    pool.tensor_tensor(yo[:], yo[:], x3[nxt][:], ALU.add).then_inc(y_ready, 1)

                if "F" in st:
                    scale_values(s - 1, 5, 1, nxt)
                if "Y" in st:
                    output()
                if "A" in st:
                    scale_values(s, 0, 0, par)
                if "F" in st:
                    square()
                if "A" in st:
                    scale_values(s, 1, 1, par)
                if "F" in st:
                    norm3()
                if "A" in st:
                    scale_values(s, 2, 0, par)
                if not isinstance(s, int) or s + 2 < B:
                    normalise(s + 2, par)
                if "A" in st:
                    for g in range(3, 5):
                        scale_values(s, g, g % 2, par)

            run_steps(pool, step)


_ORDER = ["x", "conv_w", "conv_p", "out_w", "ln_g", "ln_b", "w_in", "gate_b", "w_fin", "fin_b", "experts",
          "proj_w", "proj_b", "scale", "c_ident", "c_sel", "c_sum", "c_pat", "c_score", "c_bias"]


def kernel(**a):
    import numpy as np
    import concourse.bacc as bacc
    from concourse.bass_utils import run_bass_kernel_spmd

    f = {k: np.ascontiguousarray(v) for k, v in a.items()}
    z = lambda *s: np.zeros(s, np.float32)
    conv = z(BC, BLOCKS * TAPS, BC)
    ow = z(BC + 1, B * C)
    cwt = f["L0_tok_conv_w"].transpose(2, 0, 3, 1).reshape(CH, BLOCKS * TAPS, CH)
    for b in range(B):
        conv[CH * b:CH * b + CH, :, CH * b:CH * b + CH] = cwt
        ow[CH * b:CH * b + CH, C * b:C * b + C] = f["L0_tok_out_w"][:, :, 0].T
        ow[BC, C * b:C * b + C] = f["L0_tok_out_b"]
    par = np.stack([f["L0_tok_conv_b"], f["L0_tok_bn_gamma"], f["L0_tok_bn_beta"], f["L0_tok_bn_mean"],
                    f["L0_tok_bn_var"]])
    cp = np.ascontiguousarray(np.tile(par.transpose(2, 0, 1), (2 * B, 1, 1)))
    w_in = np.ascontiguousarray(np.concatenate([f["L0_attn_W_qkv"], f["L0_attn_W_gate"]]).T)
    experts = f["L0_ffn_weight"][0].transpose(0, 2, 1).reshape(E, PAIRS, 2, C).transpose(0, 2, 1, 3).reshape(E, 2, PAIRS * C)
    ident = np.eye(128, dtype=np.float16)
    sel = np.zeros((128, LOOKS, PAIRS), np.float16)
    for r in range(LOOKS):
        for j in range(2):
            sel[64 * j:64 * j + 64, r, 2 * r + j] = 1
    sums = np.tile(np.eye(PAIRS, dtype=np.float32), (4, 1))
    bit = ((np.arange(PATTERNS)[None, :] >> np.arange(E)[:, None]) & 1).astype(np.float32)
    score = (2 * (2 * bit - 1)).astype(np.float16)
    bias = (-(2 * bit - 1).sum(0) - (E - 1)).reshape(2, 128).T
    given = {
        "x": f["x"].reshape(BC, N), "conv_w": conv, "conv_p": cp, "out_w": ow, "ln_g": f["L0_attn_ln_gamma"],
        "ln_b": f["L0_attn_ln_beta"], "w_in": w_in, "gate_b": f["L0_attn_b_gate"].reshape(HG, 128).T,
        "w_fin": f["L0_attn_W_final"].T.reshape(HG, 128, C).transpose(1, 0, 2), "fin_b": f["L0_attn_b_final"],
        "experts": experts, "proj_w": f["L0_ffn_proj_w"].T, "proj_b": f["L0_ffn_proj_b"].reshape(E, 1),
        "scale": f["L0_ffn_scale"].reshape(C), "c_ident": ident, "c_sel": sel, "c_sum": sums, "c_pat": bit,
        "c_score": score, "c_bias": bias.astype(np.float32),
    }
    nc = bacc.Bacc("TRN2", target_bir_lowering=False, num_devices=1)
    arrays, args = {}, []
    for name in _ORDER:
        v = np.ascontiguousarray(given[name])
        arrays[f"in_{name}"] = v
        args.append(nc.dram_tensor(f"in_{name}", v.shape, mybir.dt.from_np(v.dtype), kind="ExternalInput").ap())
    args.append(nc.dram_tensor("out_0", (B, N, C), F32, kind="ExternalOutput").ap())
    build(nc, *args)
    r = run_bass_kernel_spmd(nc, [arrays], core_ids=[0])
    return r.results[0]["out_0"]
```

```python
from contextlib import ExitStack

import concourse.bass as bass
from concourse import mybir

F32 = mybir.dt.float32
F16 = mybir.dt.float16
ALU = mybir.AluOpType
ACT = mybir.ActivationFunctionType
AX = mybir.AxisListType

B, CH, N = 16, 4, 375
BLOCKS, TAPS = 9, 3
C = 64
HEADS, D = 8, 32
INNER = HEADS * D
TP, TT = 125, 3
TPAD = TP + 1
HG = 2
E, PATTERNS = 8, 256
PAIRS = C // 2
LOOKS = PAIRS // 2
EPS = 1e-5
SCALE = float(D) ** -0.5
BASE = 256.0
ROUND = 1.5 * 2.0 ** 23
BC = B * CH
CUT = 188
FIRST = 2
TABLE_AHEAD = 16
GROUPS = HG * TT
BANKS = 3
SLOTS = 3

TENSOR = """
    scores packed attend sum tokT one0   scores one1 q0   scores k0 look0 q1 k1   scores final look1
    scores look2 gate0 attend look3   scores look4 gate1 attend   scores look5 v0 look6 look7
    scores v1 look8 attend v2 sgnT   scores look9 look10 attend   scores look11
    scores look12 logit look13 look14 look15   scores attend
    """.split()
SCALAR = """
    packed   exp   exp one0   exp   exp one1   exp q0 k0   exp q1   exp   exp k1   exp gate0   exp   exp
    exp sign gate1   exp v0   exp   exp v1   exp v2 sgnT   exp   exp   exp   exp   exp   exp   exp   exp
    """.split()
VECTOR = """
    inverse   max   max sum tokT   max inverse gate_old   max q0 k0 look0   max q1 k1 final
    max inverse look1 look2 variance look3   max inverse look4 look5   max look6 look7 look8
    max inverse gate_new   max look9 look10   max look11 look12 logit inverse   max look13 look14 look15
    """.split()
GPSIMD = """
    values values output square values norm values values next1 next2 next3 values next4
    """.split()
USES = [n for n in TENSOR if n not in ("scores", "attend")]
STAGE = {"tokT": "P", "q0": "P", "q1": "P", "k0": "P", "k1": "P", "gate0": "P", "gate1": "P",
         "v0": "P", "v1": "P", "v2": "P", "final": "F", "sgnT": "F", "logit": "F", "one0": "X", "one1": "X",
         "packed": "Y", "sum": "Y"}
STAGE.update({f"look{i}": "X" for i in range(LOOKS)})
FREED_BY_ACT = {"packed", "gate0", "gate1", "sgnT", "one0", "one1", "v0", "v1", "v2"}
HALVES = TENSOR.count("scores")
QK = [n for n in USES if n in ("q0", "q1", "k0", "k1")]


def uses_of(stages):
    return [n for n in USES if STAGE[n] in stages]


class Ring:

    def __init__(self, stages, used, by_act, by_dve, phase, before):
        self.names, self.used, self.by_act, self.by_dve, self.phase = uses_of(stages), used, by_act, by_dve, phase
        self.before = before

    def bank(self, name):
        return (self.names.index(name) + self.phase) % BANKS

    def filled(self, name):
        return self.used + self.names.index(name) + 1

    def freed(self, name):
        i = self.names.index(name)
        act = name in FREED_BY_ACT
        n = sum((x in FREED_BY_ACT) == act for x in self.names[:i + 1])
        return (self.by_act if act else self.by_dve) + n

    def previous(self, name):
        i = self.names.index(name)
        if i >= BANKS:
            p = self.names[i - BANKS]
            return p in FREED_BY_ACT, self.freed(p)
        k = len(self.before) + i - BANKS
        if k < 0:
            return None
        act = self.before[k] in FREED_BY_ACT
        n = sum((x in FREED_BY_ACT) == act for x in self.before[k + 1:])
        return act, (self.by_act if act else self.by_dve) - n


def build(nc, x, conv_w, conv_p, out_w, ln_g, ln_b, w_in, gate_b, w_fin, fin_b, experts, proj_w, proj_b,
          scale, c_ident, c_sel, c_sum, c_pat, c_score, c_bias, out):
    with ExitStack() as ctx:
        def sb(name, shape, dt=F32):
            return ctx.enter_context(nc.sbuf_tensor(name, shape, dt))

        def psum(name, shape, dt=F32):
            return ctx.enter_context(nc.psum_tensor(name, shape, dt))

        def sem(name):
            return ctx.enter_context(nc.semaphore(name))

        scores = psum("scores", [128, 2, 2, 512])
        attend = psum("attend", [128, 512])
        work = psum("work", [128, BANKS, 512])

        cw = sb("cw", [BC, BLOCKS * TAPS, BC])
        cp = sb("cp", [128, 5, BLOCKS])
        bn_s = sb("bn_s", [BC, BLOCKS])
        bn_t = sb("bn_t", [BC, BLOCKS])
        ow = sb("ow", [BC + 1, B * C])
        lng = sb("lng", [TP, C])
        lnb = sb("lnb", [TP, C])
        finb = sb("finb", [TP, C])
        scl = sb("scl", [TP, C])
        w32 = sb("w32", [128, 4 * INNER])
        wh = sb("wh", [128, 4 * INNER], F16)
        wl = sb("wl", [128, 4 * INNER], F16)
        gb = sb("gb", [128, HG])
        gbh = sb("gbh", [128, HG])
        wf = sb("wf", [128, HG, C])
        wfh = sb("wfh", [128, HG, C])
        ex = sb("ex", [E, 2, PAIRS * C])
        pw32 = sb("pw32", [128, E])
        pwh = sb("pwh", [128, E], F16)
        pwl = sb("pwl", [128, E], F16)
        pb = sb("pb", [E, 1])
        ident = sb("ident", [128, 128], F16)
        sel = sb("sel", [128, LOOKS, PAIRS], F16)
        sums = sb("sums", [128, PAIRS])
        pat = sb("pat", [E, PATTERNS])
        score = sb("score", [E, PATTERNS], F16)
        sbias = sb("sbias", [128, 2])
        half = sb("half", [128, 48])
        xa = [sb(f"xa{i}", [BC + 1, N]) for i in range(2)]
        xt = sb("xt", [BC, N])
        hr = sb("hr", [BC, N])
        H = sb("H", [TP, B, TT, C])
        cen = sb("cen", [TP, B, TT, C])
        sq = sb("sq", [TP, B, TT, C])
        stat = sb("stat", [TP, 6, B, TT])
        sg = sb("sg", [128, 2, 2, PAIRS * C], F16)
        table = sb("table", [128, 2, PAIRS * C], F16)
        zn = sb("zn", [TP, 2, TT, C])
        tmp = sb("tmp", [TP, TT, C])
        zsp = [sb(f"zsp{i}", [TP, 2, TT, 2, C], F16) for i in range(2)]
        znT = sb("znT", [128, 2, N], F16)
        qk = sb("qk", [128, 4, HG, N], F16)
        stack = [sb(f"stack{i}", [128, 2, 4, HG, N], F16) for i in range(2)]
        vv = [sb(f"vv{i}", [TP, TT, INNER]) for i in range(2)]
        gate = [sb(f"gate{i}", [128, HG, N]) for i in range(2)]
        mx = sb("mx", [TP, SLOTS, 4])
        probs = sb("probs", [TP, SLOTS, 4, N])
        rs = sb("rs", [TP, SLOTS, 4])
        ri = sb("ri", [TP, SLOTS, 4])
        vn = sb("vn", [TP, SLOTS, 4, D])
        att = sb("att", [128, HG, N])
        x3 = [sb(f"x3_{i}", [TP, TT, C]) for i in range(2)]
        c3 = sb("c3", [TP, TT, C])
        q3 = sb("q3", [TP, TT, C])
        z3 = sb("z3", [TP, TT, C])
        st3 = sb("st3", [TP, 4, TT])
        zsg = sb("zsg", [TP, 2, TT, 2, C], F16)
        zxT = [sb(f"zxT{i}", [128, 2, N], F16) for i in range(2)]
        bits = sb("bits", [E, N], F16)
        onehot = sb("onehot", [128, 2, N], F16)
        prod = sb("prod", [128, LOOKS, N], F16)
        pk = sb("pk", [128, N])
        dig = sb("dig", [TP, TT, PAIRS])
        yy = sb("yy", [TP, TT, PAIRS, 2])
        yo = sb("yo", [TP, TT, C])

        ld_conv, ld_x, ld_ow, ld_ex, ld_w, ld_c = (sem(n) for n in ("ld_conv", "ld_x", "ld_ow", "ld_ex", "ld_w", "ld_c"))
        consts_set = sem("consts_set")
        ones_set = sem("ones_set")
        bn_ready = sem("bn_ready")
        conv_done = sem("conv_done")
        relu_lo, relu_hi = sem("relu_lo"), sem("relu_hi")
        shifted = sem("shifted")
        x_ready = sem("x_ready")
        h_done = sem("h_done")
        h_copied_v, h_copied_a = sem("h_copied_v"), sem("h_copied_a")
        tab_done, sg_ready = sem("tab_done"), sem("sg_ready")
        tab_ready = sem("tab_ready")
        w_high, w_ready = sem("w_high"), sem("w_ready")
        ln_v, ln_a, ln_p = sem("ln_v"), sem("ln_a"), sem("ln_p")
        work_full, work_act, work_dve = sem("work_full"), sem("work_act"), sem("work_dve")
        zn_ready, pool_link = sem("zn_ready"), sem("pool_link")
        high_ready, stacked = sem("high_ready"), sem("stacked")
        scored, max_ready, exp_done = sem("scored"), sem("max_ready"), sem("exp_done")
        sum_inverse, v_ready, av_done, gated = sem("sum_inverse"), sem("v_ready"), sem("av_done"), sem("gated")
        cen_ready, sq_ready, var_ready, split_ready, sign_ready = (
            sem("cen_ready"), sem("sq_ready"), sem("var_ready"), sem("split_ready"), sem("sign_ready"))
        cen_sum, norm_link, out_link = sem("cen_sum"), sem("norm_link"), sem("out_link")
        digits, y_ready, stored = sem("digits"), sem("y_ready"), sem("stored")

        block = ctx.enter_context(nc.Block())

        STEPS = B + 3
        LOOP0, LOOP1 = 4, 14

        def stages(s):
            on = {"P": 0 <= s + 1 < B, "F": 0 <= s - 1 < B, "X": 0 <= s - 2 < B, "Y": 0 <= s - 3 < B}
            return "".join(k for k in on if on[k])

        full = uses_of("PFXY")
        per_act = sum(n in FREED_BY_ACT for n in full)
        per_dve = len(full) - per_act
        assert len(full) % BANKS == 0

        def run_steps(eng, step):
            used = by_act = by_dve = 0
            before = []
            s = -1
            while s < STEPS:
                st = stages(s)
                names = uses_of(st)
                if s == LOOP0:
                    turns = (LOOP1 - LOOP0) // 2
                    with eng.Fori(0, turns) as j:
                        for k in range(2):
                            ring = Ring(st, j * (2 * len(full)) + (used + k * len(full)),
                                        j * (2 * per_act) + (by_act + k * per_act),
                                        j * (2 * per_dve) + (by_dve + k * per_dve),
                                        used % BANKS, before[-BANKS:] if k == 0 else names[-BANKS:])
                            step(j * 2 + (s + k), (s + k) % 2, st + "A", ring)
                    used, by_act, by_dve = (used + 2 * turns * len(full), by_act + 2 * turns * per_act,
                                            by_dve + 2 * turns * per_dve)
                    s = LOOP1
                else:
                    step(s, s % 2, st + ("A" if 0 <= s < B else ""),
                         Ring(st, used, by_act, by_dve, used % BANKS, before[-BANKS:]))
                    used += len(names)
                    by_act += sum(n in FREED_BY_ACT for n in names)
                    by_dve += sum(n not in FREED_BY_ACT for n in names)
                    s += 1
                before = before + names

        def transposed_tiles(bank):
            return work[:, bank, :].bitcast(F16)[:, 0:2 * TT * TPAD].rearrange("p (i n) -> p i n", n=TPAD)[:, :, 0:TP]

        def table_bank(i):
            return attend[:] if i % 2 else scores[:, 1, 1, :]

        PARTS = ((0, FIRST), (FIRST, 9), (9, B))

        def part_bank(i, t):
            lo, hi = PARTS[i]
            n = C * (hi - lo)
            if i == 0:
                return work[0:TP, 0, n * t:n * t + n]
            return (scores[0:TP, t // 2, t % 2, 0:n], work[0:TP, t, 0:n])[i - 1]


        def at(s, k):
            return isinstance(s, int) and s == k

        def geq(eng, semaphore, count):
            if not isinstance(count, int) or count > 0:
                eng.wait_ge(semaphore, count)

        @block.sync
        def _(sp):
            sp.dma_start(xa[0][0:BC, :], x).then_inc(ld_x, 16)
            sp.dma_start(cp[:], conv_p).then_inc(ld_conv, 16)
            sp.dma_start(cw[:], conv_w).then_inc(ld_conv, 16)
            sp.dma_start(pat[:], c_pat).then_inc(ld_ex, 16)
            sp.dma_start(ex[:], experts).then_inc(ld_ex, 16)
            sp.dma_start(ow[:], out_w).then_inc(ld_ow, 16)
            for r in range(2):
                sp.dma_start(w32[C * r:C * r + C, :], w_in).then_inc(ld_w, 16)
                sp.dma_start(pw32[C * r:C * r + C, :], proj_w).then_inc(ld_w, 16)
            sp.dma_start(wf[:], w_fin).then_inc(ld_w, 16)
            sp.dma_start(gb[:], gate_b).then_inc(ld_w, 16)
            for dst, src in ((ident, c_ident), (sel, c_sel), (sums, c_sum), (score, c_score), (sbias, c_bias),
                             (pb, proj_b)):
                sp.dma_start(dst[:], src).then_inc(ld_c, 16)
            for dst, src in ((lng, ln_g), (lnb, ln_b), (finb, fin_b), (scl, scale)):
                sp.dma_start(dst[:], src.partition_broadcast(TP)).then_inc(ld_c, 16)

            def step(s, par, st, ring):
                if "Y" in st:
                    dst = out[s - 3:s - 2] if isinstance(s, int) else out[bass.ds(sp.snap(s - 3), 1)]
                    sp.wait_ge(y_ready, s - 3 + 1)
                    sp.dma_start(dst.rearrange("o (p t) c -> (o p) t c", t=TT), yo[:]).then_inc(stored, 16)
                if "P" in st:
                    b = s + 1
                    sp.wait_ge(work_dve, ring.freed("k1"))
                    geq(sp, stacked, 256 * b)
                    for r in range(4):
                        qi, ki = r // 2, 2 + r % 2
                        for h in range(4):
                            sp.dma_start(stack[1 - par][D * r:D * r + D, :, h, :, :],
                                         qk[D * h:D * h + D, qi:ki + 1:ki - qi, :, :]).then_inc(stacked, 16)

            run_steps(sp, step)
            sp.wait_ge(stored, 16 * B)

        @block.tensor
        def _(pe):
            def table_mm(i):
                k, c = i // 2, 256 * (i % 2)
                if i == 0:
                    pe.wait_ge(ld_ex, 32)
                if i % 2 == 0 and k >= 2:
                    pe.wait_ge(sg_ready, k - 1)
                hp, dg, ch = k // 8, k // 4 % 2, k % 4
                pe.matmul(table_bank(k)[:, c:c + 256], pat[:, 128 * hp:128 * hp + 128],
                          ex[:, dg, 512 * ch + c:512 * ch + c + 256], start=True, stop=True).then_inc(tab_done, 1)

            pe.wait_ge(ld_conv, 32)
            pe.wait_ge(ld_x, 16)
            for n in range(BLOCKS):
                d = 2 ** n
                geq(pe, x_ready, n)
                cur = xa[n % 2]
                cuts = ((0, CUT), (CUT, N))
                spans = [[(k, max(lo, (2 - k) * d), hi) for k in (2, 1, 0) if max(lo, (2 - k) * d) < hi] for lo, hi in cuts]
                for t in range(TAPS):
                    for c in range(2):
                        if t >= len(spans[c]):
                            continue
                        k, lo, hi = spans[c][t]
                        sh = (2 - k) * d
                        mm = pe.matmul(scores[BC * c:BC * c + BC, n % 2, 0, lo - cuts[c][0]:hi - cuts[c][0]],
                                       cw[:, n * TAPS + k, :], cur[0:BC, lo - sh:hi - sh],
                                       start=(t == 0), stop=(t == len(spans[c]) - 1), skip_group_check=True)
                mm.then_inc(conv_done, 1)
                table_mm(n)
            pe.wait_ge(x_ready, BLOCKS)
            pe.wait_ge(ones_set, 2)
            pe.wait_ge(ld_ow, 16)
            for i, (lo, hi) in enumerate(PARTS):
                for t in range(TT):
                    if i == 2 and t == 0:
                        pe.wait_ge(h_copied_v, 1)
                    mm = pe.matmul(part_bank(i, t), xa[BLOCKS % 2][:, t:N:TT], ow[:, C * lo:C * hi], start=True, stop=True)
                    if i > 0 or t == TT - 1:
                        mm.then_inc(h_done, 1)
            for i in range(BLOCKS, TABLE_AHEAD):
                table_mm(i)
            pe.wait_ge(w_ready, 5)
            pe.wait_ge(ld_c, 160)
            pe.wait_ge(h_copied_a, 2 * TT)

            def step(s, par, st, ring):
                nxt = 1 - par

                def open_bank(name):
                    prev = ring.previous(name)
                    if prev:
                        pe.wait_ge(work_act if prev[0] else work_dve, prev[1])
                    return work[:, ring.bank(name), :]

                def tokT():
                    pe.wait_ge(zn_ready, s + 2)
                    o = open_bank("tokT").bitcast(F16)
                    for i in range(2):
                        for t in range(TT):
                            mm = pe.transpose(o[:, TPAD * (TT * i + t):TPAD * (TT * i + t) + TP],
                                              zsp[nxt][:, i, t, :, :].rearrange("p a c -> p (a c)"), ident[0:TP, 0:TP])
                    mm.then_inc(work_full, 1)

                def feature_major(name, col, src):
                    if name == "q0":
                        pe.wait_ge(work_dve, ring.freed("tokT"))
                    o = open_bank(name)
                    pe.matmul(o[:, 0:N], wh[:, col:col + 128], znT[:, src, :], start=True, stop=False)
                    pe.matmul(o[:, 0:N], wl[:, col:col + 128], znT[:, src, :], start=False, stop=True).then_inc(work_full, 1)

                def token_major(t):
                    o = open_bank(f"v{t}")
                    for w in (wh, wl):
                        mm = pe.matmul(o[0:TP, 0:INNER], znT[:, 1, TP * t:TP * t + TP], w[:, 2 * INNER:3 * INNER],
                                       start=(w is wh), stop=(w is wl))
                    mm.then_inc(work_full, 1)

                def final():
                    pe.wait_ge(gated, 2 * (s - 1) + 2)
                    o = open_bank("final")
                    for t in range(TT):
                        for g in range(HG):
                            mm = pe.matmul(o[0:TP, C * t:C * t + C], att[:, g, TP * t:TP * t + TP], wfh[:, g, :],
                                           start=(g == 0), stop=(g == HG - 1))
                    mm.then_inc(work_full, 1)

                def sgnT():
                    pe.wait_ge(split_ready, s)
                    pe.wait_ge(sign_ready, s)
                    o = open_bank("sgnT").bitcast(F16)
                    for i in range(2):
                        for t in range(TT):
                            mm = pe.transpose(o[:, TPAD * (TT * i + t):TPAD * (TT * i + t) + TP],
                                              zsg[:, i, t, :, :].rearrange("p a c -> p (a c)"), ident[0:TP, 0:TP])
                    mm.then_inc(work_full, 1)

                def logit():
                    pe.wait_ge(work_act, ring.freed("sgnT"))
                    o = open_bank("logit")
                    pe.matmul(o[0:E, 0:N], pwh[:], zxT[nxt][:, 0, :], start=True, stop=False)
                    pe.matmul(o[0:E, 0:N], pwl[:], zxT[nxt][:, 0, :], start=False, stop=True).then_inc(work_full, 1)

                def one(i):
                    if i == 0:
                        pe.wait_ge(work_dve, ring.by_dve)
                    o = open_bank(f"one{i}")
                    pe.matmul(o[:, 0:N], score[:, 128 * i:128 * i + 128], bits[:], start=True,
                              stop=True).then_inc(work_full, 1)

                def look(r):
                    if r == 0:
                        pe.wait_ge(work_act, ring.freed("one1"))
                    o = open_bank(f"look{r}")
                    pe.matmul(o[:, 0:N], table[:, 0, 128 * r:128 * r + 128], onehot[:, 0, :], start=True, stop=False)
                    pe.matmul(o[:, 0:N], table[:, 1, 128 * r:128 * r + 128], onehot[:, 1, :], start=False,
                              stop=True).then_inc(work_full, 1)

                def reduce():
                    o = open_bank("packed")
                    pe.wait_ge(work_dve, ring.by_dve)
                    for r in range(LOOKS):
                        c = r % 4
                        mm = pe.matmul(o[32 * c:32 * c + 32, 0:N], sel[:, r, :], prod[:, r, :], start=(r < 4),
                                       stop=(r >= LOOKS - 4), skip_group_check=True)
                    mm.then_inc(work_full, 1)

                def total():
                    pe.wait_ge(work_act, ring.freed("packed"))
                    o = open_bank("sum")
                    for t in range(TT):
                        mm = pe.matmul(o[0:TP, PAIRS * t:PAIRS * t + PAIRS], pk[:, TP * t:TP * t + TP], sums[:],
                                       start=True, stop=True)
                    mm.then_inc(work_full, 1)

                def sum_queries(b, g):
                    pe.wait_ge(v_ready, 6 * b + g + 1)
                    if g % TT == 0:
                        geq(pe, gated, 2 * b + g // TT)
                    for h in range(4):
                        mm = pe.matmul(attend[32 * h:32 * h + 32, 0:N], vn[:, g % SLOTS, h, :], probs[:, g % SLOTS, h, :],
                                       start=(g % TT == 0), stop=(g % TT == TT - 1), skip_group_check=True)
                    mm.then_inc(av_done, 1)

                todo = {"tokT": tokT, "q0": lambda: feature_major("q0", 0, 1), "q1": lambda: feature_major("q1", 128, 1),
                        "k0": lambda: feature_major("k0", INNER, 1), "k1": lambda: feature_major("k1", INNER + 128, 1),
                        "gate0": lambda: feature_major("gate0", 3 * INNER, 0),
                        "gate1": lambda: feature_major("gate1", 3 * INNER + 128, 0),
                        "v0": lambda: token_major(0), "v1": lambda: token_major(1), "v2": lambda: token_major(2),
                        "final": final, "sgnT": sgnT, "logit": logit, "one0": lambda: one(0), "one1": lambda: one(1),
                        "packed": reduce, "sum": total}
                for r in range(LOOKS):
                    todo[f"look{r}"] = lambda r=r: look(r)

                def scores_of(b, h, slots):
                    geq(pe, exp_done, 2 * (12 * b + h) - 2)
                    hg, t, p = h // 2 // TT, h // 2 % TT, h % 2
                    for i in range(2):
                        mm = pe.matmul(scores[0:TP, p, i, 0:N], slots[:, 0, 2 * p + i, hg, TP * t:TP * t + TP],
                                       slots[:, 1, 2 * p + i, hg, :], start=True, stop=True)
                    mm.then_inc(scored, 1)

                h = g = 0
                if at(s, 0):
                    pe.wait_ge(sg_ready, 16)
                if at(s, 2):
                    pe.wait_ge(tab_ready, 4)
                for name in TENSOR:
                    if name == "scores":
                        h += 1
                        if h < HALVES and "A" in st:
                            scores_of(s, h, stack[par])
                        if at(s, -1) and h == HALVES:
                            for i in range(TABLE_AHEAD, 32):
                                table_mm(i)
                        if h == HALVES and "P" in st:
                            pe.wait_ge(stacked, 256 * (s + 2))
                            scores_of(s + 1, 0, stack[nxt])
                    elif name == "attend":
                        if g == 0 and "F" in st:
                            sum_queries(s - 1, GROUPS - 1)
                        if g > 0 and "A" in st:
                            sum_queries(s, g - 1)
                        g += 1
                    elif STAGE[name] in st:
                        todo[name]()

            run_steps(pe, step)

        @block.scalar
        def _(act):
            def table_sign(i):
                act.wait_ge(tab_done, 2 * i + 2)
                hp, dg, ch = i // 8, i // 4 % 2, i % 4
                act.activation(sg[:, hp, dg, 512 * ch:512 * ch + 512], table_bank(i),
                               ACT.Sign).then_inc(sg_ready, 1)

            act.wait_ge(ld_conv, 32)
            for n in range(BLOCKS):
                act.wait_ge(conv_done, n + 1)
                act.activation(hr[:, CUT:N], scores[BC:2 * BC, n % 2, 0, 0:N - CUT], ACT.Relu,
                               bias=cp[BC:2 * BC, 0, n:n + 1]).then_inc(relu_hi, 1)
                if n % 2 == 1:
                    table_sign(n // 2)
                if n == 4:
                    act.wait_ge(ld_w, 96)
                    act.activation(wh[:], w32[:], ACT.Copy).then_inc(w_high, 1)
            for i in (1, 2):
                lo, hi = PARTS[i]
                for t in range(TT):
                    act.wait_ge(h_done, TT * (i - 1) + t + 2)
                    act.activation(H[:, lo:hi, t, :], part_bank(i, t).rearrange("p (b c) -> p b c", c=C),
                                   ACT.Copy).then_inc(h_copied_a, 1)
            for i in range(BLOCKS // 2, TABLE_AHEAD // 2):
                table_sign(i)
            act.wait_ge(ln_v, 6)
            act.activation(sq[:, FIRST:].rearrange("p b t c -> p (b t c)"), cen[:, FIRST:].rearrange("p b t c -> p (b t c)"),
                           ACT.Square).then_inc(ln_a, 1)

            def step(s, par, st, ring):
                nxt = 1 - par

                def high(i):
                    name = ("q0", "q1", "k0", "k1")[i]
                    if name == QK[0]:
                        geq(act, stacked, 256 * (s + 1))
                    act.wait_ge(work_full, ring.filled(name))
                    act.activation(qk[:, 2 * (i // 2), i % 2, :], work[:, ring.bank(name), 0:N], ACT.Copy,
                                   scale=(-SCALE if i < 2 else 1.0)).then_inc(high_ready, 1)

                def gates(i):
                    name = f"gate{i}"
                    if i == 0:
                        geq(act, gated, 2 * s)
                    act.wait_ge(work_full, ring.filled(name))
                    act.activation(gate[nxt][:, i, :], work[:, ring.bank(name), 0:N], ACT.Tanh, bias=gbh[:, i:i + 1],
                                   scale=0.5).then_inc(work_act, 1)

                def values(t):
                    if t == 0:
                        geq(act, v_ready, 6 * s)
                    act.wait_ge(work_full, ring.filled(f"v{t}"))
                    act.activation(vv[nxt][:, t, :], work[0:TP, ring.bank(f"v{t}"), 0:INNER],
                                   ACT.Copy).then_inc(work_act, 1)

                def sign():
                    act.wait_ge(cen_ready, s)
                    for r in range(2):
                        a = act.activation(zsg[:, 1, :, r, :], c3[:], ACT.Sign)
                    a.then_inc(sign_ready, 1)

                def transposed():
                    act.wait_ge(work_full, ring.filled("sgnT"))
                    act.activation(zxT[nxt][:].rearrange("p a (t n) -> p (a t) n", t=TT),
                                   transposed_tiles(ring.bank("sgnT")), ACT.Copy).then_inc(work_act, 1)

                def one(i):
                    name = f"one{i}"
                    act.wait_ge(work_full, ring.filled(name))
                    act.activation(onehot[:, i, :], work[:, ring.bank(name), 0:N], ACT.Relu,
                                   bias=sbias[:, i:i + 1]).then_inc(work_act, 1)

                def copy_packed():
                    act.wait_ge(work_full, ring.filled("packed"))
                    act.activation(pk[:], work[:, ring.bank("packed"), 0:N], ACT.Copy).then_inc(work_act, 1)

                todo = {"q0": lambda: high(0), "q1": lambda: high(1), "k0": lambda: high(2), "k1": lambda: high(3),
                        "gate0": lambda: gates(0), "gate1": lambda: gates(1), "v0": lambda: values(0),
                        "v1": lambda: values(1), "v2": lambda: values(2), "sgnT": transposed, "one0": lambda: one(0),
                        "one1": lambda: one(1), "packed": copy_packed}

                def exponential(k):
                    h, g, i = k // 2, k // 4, k % 4
                    if k % 2 == 0:
                        act.wait_ge(max_ready, 12 * s + h + 1)
                    if i == 0:
                        geq(act, av_done, 6 * s + g - SLOTS + 1)
                    act.activation(probs[:, g % SLOTS, i, :], scores[0:TP, h % 2, i % 2, 0:N], ACT.Exp, scale=-1.0,
                                   bias=mx[:, g % SLOTS, i:i + 1],
                                   accum_out=rs[:, g % SLOTS, i:i + 1]).then_inc(exp_done, 1)

                k = 0
                for name in SCALAR:
                    if name == "exp":
                        if "A" in st:
                            exponential(k)
                        k += 1
                    elif name == "sign":
                        if "F" in st:
                            sign()
                    elif STAGE[name] in st:
                        todo[name]()
                if at(s, -1):
                    for i in range(TABLE_AHEAD // 2, 16):
                        table_sign(i)

            run_steps(act, step)

        @block.vector
        def _(dve):
            for i in range(2):
                dve.memset(xa[i][BC:BC + 1, :], 1.0).then_inc(ones_set, 1)
            dve.wait_ge(ld_conv, 32)
            for n in range(BLOCKS):
                cur, new = xa[n % 2], xa[(n + 1) % 2]
                dve.wait_ge(conv_done, n + 1)
                dve.tensor_scalar(hr[:, 0:CUT], scores[0:BC, n % 2, 0, 0:CUT], cp[0:BC, 0, n:n + 1], 0.0,
                                  ALU.add, ALU.max).then_inc(relu_lo, 1)
                dve.wait_ge(relu_lo, n + 1)
                dve.wait_ge(relu_hi, n + 1)
                dve.wait_ge(shifted, n + 1)
                dve.scalar_tensor_tensor(new[0:BC, :], hr[:], bn_s[:, n:n + 1], xt[:], ALU.mult, ALU.add).then_inc(x_ready, 1)
                if n == 4:
                    dve.wait_ge(w_high, 1)
                    dve.tensor_tensor(wl[:], w32[:], wh[:], ALU.subtract).then_inc(w_ready, 1)
                if n == 5:
                    dve.tensor_copy(pwh[:], pw32[:]).then_inc(w_ready, 1)
                    dve.wait_ge(w_ready, 2)
                    dve.tensor_tensor(pwl[:], pw32[:], pwh[:], ALU.subtract).then_inc(w_ready, 1)
                if n == 6:
                    dve.tensor_scalar(gbh[:], gb[:], 0.5, None, ALU.mult).then_inc(w_ready, 1)
                    dve.tensor_scalar(wfh[:], wf[:], 0.5, None, ALU.mult).then_inc(w_ready, 1)
            s1, v1 = stat[:, 0], stat[:, 1]
            lo, hi = PARTS[0]
            dve.wait_ge(h_done, 1)
            dve.tensor_copy(H[:, lo:hi].rearrange("p b t c -> p t b c"),
                            work[0:TP, 0, 0:TT * C * (hi - lo)].rearrange("p (t b c) -> p t b c", t=TT, c=C)).then_inc(h_copied_v, 1)
            dve.wait_ge(h_copied_v, 1)

            def centre(lo, hi, k):
                n = TT * (hi - lo)
                dve.tensor_reduce(s1[:, lo:hi], H[:, lo:hi], AX.X, ALU.add).then_inc(ln_v, 1)
                dve.wait_ge(ln_v, k + 1)
                dve.scalar_tensor_tensor(cen[:, lo:hi].rearrange("p b t c -> p (b t) c"),
                                         s1[:, lo:hi].rearrange("p b t -> p (b t)").unsqueeze(2).to_broadcast([TP, n, C]), -1.0 / C,
                                         H[:, lo:hi].rearrange("p b t c -> p (b t) c"), ALU.mult, ALU.add).then_inc(ln_v, 1)

            centre(lo, hi, 0)
            dve.wait_ge(ln_v, 2)
            dve.tensor_tensor(sq[:, lo:hi], cen[:, lo:hi], cen[:, lo:hi], ALU.mult).then_inc(ln_v, 1)
            dve.wait_ge(ln_v, 3)
            dve.tensor_reduce(v1[:, lo:hi], sq[:, lo:hi], AX.X, ALU.add).then_inc(ln_v, 1)
            dve.wait_ge(h_copied_a, 2 * TT)
            centre(FIRST, B, 4)
            dve.wait_ge(ld_c, 160)

            def table_part(i):
                if i == 0:
                    dve.wait_ge(sg_ready, 16)
                hp, c = i // 2, i % 2 * (PAIRS * C // 2)
                dve.scalar_tensor_tensor(table[:, hp, c:c + PAIRS * C // 2], sg[:, hp, 1, c:c + PAIRS * C // 2], BASE,
                                         sg[:, hp, 0, c:c + PAIRS * C // 2], ALU.mult, ALU.add).then_inc(tab_ready, 1)

            def step(s, par, st, ring):
                nxt = 1 - par

                def tokT():
                    dve.wait_ge(work_full, ring.filled("tokT"))
                    dve.tensor_copy(znT[:].rearrange("p a (t n) -> p (a t) n", t=TT),
                                    transposed_tiles(ring.bank("tokT"))).then_inc(work_dve, 1)

                def low(i):
                    name = ("q0", "q1", "k0", "k1")[i]
                    dve.wait_ge(high_ready, 4 * (s + 1) + QK.index(name) + 1)
                    dve.scalar_tensor_tensor(qk[:, 2 * (i // 2) + 1, i % 2, :], work[:, ring.bank(name), 0:N],
                                             (-SCALE if i < 2 else 1.0), qk[:, 2 * (i // 2), i % 2, :], ALU.mult,
                                             ALU.subtract).then_inc(work_dve, 1)

                def final():
                    dve.wait_ge(work_full, ring.filled("final"))
                    if "Y" in st or "X" in st:
                        geq(dve, y_ready, s - 2)
                    hz = H[:, bass.ds(s - 1, 1)] if not isinstance(s, int) else H[:, s - 1:s]
                    xr = x3[nxt][:].rearrange("p t c -> p (t c)")
                    dve.tensor_tensor(xr, work[0:TP, ring.bank("final"), 0:TT * C],
                                      hz.rearrange("p o t c -> p (o t c)"), ALU.add).then_inc(work_dve, 1)
                    dve.wait_ge(work_dve, ring.freed("final"))
                    dve.tensor_reduce(st3[:, 0], x3[nxt][:], AX.X, ALU.add).then_inc(cen_sum, 1)
                    dve.wait_ge(cen_sum, s)
                    dve.scalar_tensor_tensor(c3[:], st3[:, 0].unsqueeze(2).to_broadcast([TP, TT, C]), -1.0 / C, x3[nxt][:],
                                             ALU.mult, ALU.add).then_inc(cen_ready, 1)

                def variance():
                    dve.wait_ge(sq_ready, s)
                    dve.tensor_reduce(st3[:, 1], q3[:], AX.X, ALU.add).then_inc(var_ready, 1)
                    dve.wait_ge(var_ready, 2 * (s - 1) + 1)
                    dve.tensor_scalar(st3[:, 2], st3[:, 1], 1.0 / C, EPS, ALU.mult, ALU.add).then_inc(var_ready, 1)

                def logit():
                    dve.wait_ge(work_full, ring.filled("logit"))
                    dve.tensor_scalar(bits[:], work[0:E, ring.bank("logit"), 0:N], pb[:], 0.0, ALU.add,
                                      ALU.is_gt).then_inc(work_dve, 1)

                def look(r):
                    name = f"look{r}"
                    dve.wait_ge(work_full, ring.filled(name))
                    dve.tensor_tensor(prod[:, r, :], work[:, ring.bank(name), 0:N], zxT[par][:, 1, :],
                                      ALU.mult).then_inc(work_dve, 1)

                def unpack():
                    dve.wait_ge(work_full, ring.filled("sum"))
                    geq(dve, y_ready, s - 3)
                    o = work[0:TP, ring.bank("sum"), 0:TT * PAIRS].rearrange("p (t c) -> p t c", t=TT)
                    dve.tensor_scalar(dig[:], o, 1.0 / BASE, ROUND, ALU.mult, ALU.add).then_inc(digits, 1)
                    dve.wait_ge(digits, 2 * (s - 3) + 1)
                    dve.tensor_scalar(yy[:, :, :, 1], dig[:], -ROUND, None, ALU.add).then_inc(digits, 1)
                    dve.wait_ge(digits, 2 * (s - 3) + 2)
                    dve.scalar_tensor_tensor(yy[:, :, :, 0], yy[:, :, :, 1], -BASE, o, ALU.mult, ALU.add).then_inc(work_dve, 1)

                todo = {"tokT": tokT, "q0": lambda: low(0), "q1": lambda: low(1), "k0": lambda: low(2),
                        "k1": lambda: low(3), "final": final, "logit": logit, "sum": unpack}
                for r in range(LOOKS):
                    todo[f"look{r}"] = lambda r=r: look(r)

                def inverse(b, g):
                    dve.wait_ge(exp_done, 24 * b + 4 * g + 4)
                    dve.reciprocal(ri[:, g % SLOTS, :], rs[:, g % SLOTS, :]).then_inc(sum_inverse, 1)

                def apply_gate(b, hg, which):
                    dve.wait_ge(av_done, 6 * b + TT * hg + TT)
                    dve.scalar_tensor_tensor(att[:, hg, :], gate[which][:, hg, :], 1.0, attend[:, 0:N], ALU.add,
                                             ALU.mult).then_inc(gated, 1)

                h = g = 0
                for name in VECTOR:
                    if name == "max":
                        if "A" in st:
                            dve.wait_ge(scored, 12 * s + h + 1)
                            dve.tensor_reduce(mx[:, h // 2 % SLOTS, h % 2 * 2:h % 2 * 2 + 2], scores[0:TP, h % 2, :, 0:N],
                                              AX.X, ALU.min).then_inc(max_ready, 1)
                        if at(s, 0) and 2 <= h < 6:
                            table_part(h - 2)
                        h += 1
                    elif name == "inverse":
                        if g == 0 and "F" in st:
                            inverse(s - 1, GROUPS - 1)
                        if g > 0 and "A" in st:
                            inverse(s, g - 1)
                        g += 1
                    elif name == "gate_old":
                        if "F" in st:
                            apply_gate(s - 1, 1, nxt)
                    elif name == "gate_new":
                        if "A" in st:
                            apply_gate(s, 0, par)
                    elif name == "variance":
                        if "F" in st:
                            variance()
                    elif STAGE[name] in st:
                        todo[name]()
                if at(s, -1):
                    dve.wait_ge(ln_a, 1)
                    dve.tensor_reduce(v1[:, FIRST:], sq[:, FIRST:], AX.X, ALU.add).then_inc(ln_v, 1)

            run_steps(dve, step)

        @block.gpsimd
        def _(pool):
            pool.memset(half[:], -0.5).then_inc(consts_set, 1)
            pool.wait_ge(consts_set, 1)
            pool.wait_ge(ld_conv, 32)
            pool.tensor_scalar(bn_s[:], cp[0:BC, 4, :], EPS, None, ALU.add).then_inc(bn_ready, 1)
            pool.wait_ge(bn_ready, 1)
            pool.tensor_tensor(bn_t[:], bn_s[:], half[0:BC, 0:BLOCKS], ALU.pow).then_inc(bn_ready, 1)
            pool.wait_ge(bn_ready, 2)
            pool.tensor_tensor(bn_s[:], bn_t[:], cp[0:BC, 1, :], ALU.mult).then_inc(bn_ready, 1)
            pool.wait_ge(bn_ready, 3)
            pool.tensor_tensor(bn_t[:], bn_s[:], cp[0:BC, 3, :], ALU.mult).then_inc(bn_ready, 1)
            pool.wait_ge(bn_ready, 4)
            pool.tensor_tensor(bn_t[:], cp[0:BC, 2, :], bn_t[:], ALU.subtract).then_inc(bn_ready, 1)
            pool.wait_ge(bn_ready, 5)
            pool.wait_ge(ld_x, 16)
            for n in range(BLOCKS):
                geq(pool, x_ready, n)
                pool.tensor_scalar(xt[:], xa[n % 2][0:BC, :], bn_t[:, n:n + 1], None, ALU.add).then_inc(shifted, 1)

            def deviations(lo, hi, k):
                n = TT * (hi - lo)
                v1, r1, r2, t1, t2 = (stat[:, i, lo:hi].rearrange("p b t -> p (b t)") for i in range(1, 6))
                hv = half[0:TP, 0:n]
                for i, (o, a, b, op) in enumerate(((t1, v1, None, None), (r1, t1, hv, ALU.pow), (t2, r1, r1, ALU.mult),
                                                   (t1, t2, v1, ALU.mult), (t2, t1, None, None), (r2, t2, hv, ALU.pow))):
                    if b is None:
                        ins = pool.tensor_scalar(o, a, 1.0 / C, EPS, ALU.mult, ALU.add)
                    else:
                        ins = pool.tensor_tensor(o, a, b, op)
                    ins.then_inc(ln_p, 1)
                    pool.wait_ge(ln_p, k + i + 1)

            pool.wait_ge(ln_v, 4)
            deviations(0, FIRST, 0)
            pool.wait_ge(ld_c, 160)

            def normalise(b, par, part):
                def one_b(a):
                    return a[:, bass.ds(b, 1)] if not isinstance(b, int) else a[:, b:b + 1]

                def wide(v):
                    return v.rearrange("p o t -> p (o t)").unsqueeze(2).to_broadcast([TP, TT, C])

                def rows(v):
                    return v[:].unsqueeze(1).to_broadcast([TP, TT, C])

                zt, nt = zn[:, 0], zn[:, 1]
                high = [zsp[par][:, i, :, 0, :] for i in range(2)]
                low = [zsp[par][:, i, :, 1, :] for i in range(2)]
                hb = one_b(H).rearrange("p o t c -> p (o t) c")
                k = 9 * b

                def nxt(ins):
                    ins.then_inc(pool_link, 1)

                cb, r1b = one_b(cen).rearrange("p o t c -> p (o t) c"), wide(one_b(stat[:, 2]))
                if part == 1:
                    geq(pool, pool_link, k)
                    geq(pool, zn_ready, b)
                    nxt(pool.tensor_tensor(high[0], cb, r1b, ALU.mult))
                    nxt(pool.tensor_tensor(zt, cb, r1b, ALU.mult))
                if part == 2:
                    pool.wait_ge(pool_link, k + 2)
                    nxt(pool.tensor_tensor(tmp[:], zt, wide(one_b(stat[:, 3])), ALU.mult))
                    pool.wait_ge(pool_link, k + 3)
                    nxt(pool.tensor_tensor(nt, tmp[:], rows(lng), ALU.mult))
                if part == 3:
                    pool.wait_ge(pool_link, k + 4)
                    nxt(pool.tensor_tensor(high[1], nt, rows(lnb), ALU.add))
                    nxt(pool.tensor_tensor(tmp[:], zt, rows(finb), ALU.add))
                    nxt(pool.tensor_tensor(nt, nt, rows(lnb), ALU.add))
                if part == 4:
                    pool.wait_ge(pool_link, k + 7)
                    nxt(pool.tensor_tensor(hb, hb, tmp[:], ALU.add))
                    nxt(pool.tensor_tensor(low[0], zt, high[0], ALU.subtract))
                    pool.tensor_tensor(low[1], nt, high[1], ALU.subtract).then_inc(zn_ready, 1)

            for part in range(1, 5):
                normalise(0, 0, part)

            def step(s, par, st, ring):
                nxt = 1 - par

                def scale_values(b, g, which):
                    pool.wait_ge(sum_inverse, 6 * b + g + 1)
                    geq(pool, av_done, 6 * b + g - SLOTS + 1)
                    hg, t = g // TT, g % TT
                    pool.tensor_tensor(vn[:, g % SLOTS], vv[which][:, t, 128 * hg:128 * hg + 128].rearrange("p (h d) -> p h d", d=D),
                                       ri[:, g % SLOTS, :].unsqueeze(2).to_broadcast([TP, 4, D]), ALU.mult).then_inc(v_ready, 1)

                def square():
                    pool.wait_ge(cen_ready, s)
                    pool.tensor_tensor(q3[:], c3[:], c3[:], ALU.mult).then_inc(sq_ready, 1)

                def norm3():
                    k = 3 * (s - 1)
                    pool.wait_ge(var_ready, 2 * s)
                    geq(pool, split_ready, s - 1)
                    pool.tensor_tensor(st3[:, 3], st3[:, 2], half[0:TP, 0:TT], ALU.pow).then_inc(norm_link, 1)
                    pool.wait_ge(norm_link, k + 1)
                    wide = st3[:, 3].unsqueeze(2).to_broadcast([TP, TT, C])
                    pool.tensor_tensor(zsg[:, 0, :, 0, :], c3[:], wide, ALU.mult).then_inc(norm_link, 1)
                    pool.tensor_tensor(z3[:], c3[:], wide, ALU.mult).then_inc(norm_link, 1)
                    pool.wait_ge(norm_link, k + 3)
                    pool.tensor_tensor(zsg[:, 0, :, 1, :], z3[:], zsg[:, 0, :, 0, :], ALU.subtract).then_inc(split_ready, 1)

                def output():
                    pool.wait_ge(work_dve, ring.freed("sum"))
                    geq(pool, stored, 16 * (s - 3))
                    y3 = yy[:].rearrange("p t c g -> p t (c g)")
                    pool.tensor_tensor(yo[:], y3, scl[:].unsqueeze(1).to_broadcast([TP, TT, C]), ALU.mult).then_inc(out_link, 1)
                    pool.wait_ge(out_link, s - 2)
                    pool.tensor_tensor(yo[:], yo[:], x3[nxt][:], ALU.add).then_inc(y_ready, 1)

                g = 0
                for name in GPSIMD:
                    if name == "values":
                        if g == 0 and "F" in st:
                            scale_values(s - 1, GROUPS - 1, nxt)
                        if g > 0 and "A" in st:
                            scale_values(s, g - 1, par)
                        g += 1
                    elif name == "output":
                        if "Y" in st:
                            output()
                    elif name == "square":
                        if "F" in st:
                            square()
                    elif name == "norm":
                        if "F" in st:
                            norm3()
                    elif not isinstance(s, int) or s + 2 < B:
                        normalise(s + 2, par, int(name[-1]))
                if at(s, -1):
                    pool.wait_ge(ln_v, 7)
                    deviations(FIRST, B, 6)

            run_steps(pool, step)


_ORDER = ["x", "conv_w", "conv_p", "out_w", "ln_g", "ln_b", "w_in", "gate_b", "w_fin", "fin_b", "experts",
          "proj_w", "proj_b", "scale", "c_ident", "c_sel", "c_sum", "c_pat", "c_score", "c_bias"]


def kernel(**a):
    import numpy as np
    import concourse.bacc as bacc
    from concourse.bass_utils import run_bass_kernel_spmd

    f = {k: np.ascontiguousarray(v) for k, v in a.items()}
    z = lambda *s: np.zeros(s, np.float32)
    conv = z(BC, BLOCKS * TAPS, BC)
    ow = z(BC + 1, B * C)
    cwt = f["L0_tok_conv_w"].transpose(2, 0, 3, 1).reshape(CH, BLOCKS * TAPS, CH)
    for b in range(B):
        conv[CH * b:CH * b + CH, :, CH * b:CH * b + CH] = cwt
        ow[CH * b:CH * b + CH, C * b:C * b + C] = f["L0_tok_out_w"][:, :, 0].T
        ow[BC, C * b:C * b + C] = f["L0_tok_out_b"]
    par = np.stack([f["L0_tok_conv_b"], f["L0_tok_bn_gamma"], f["L0_tok_bn_beta"], f["L0_tok_bn_mean"],
                    f["L0_tok_bn_var"]])
    cp = np.ascontiguousarray(np.tile(par.transpose(2, 0, 1), (2 * B, 1, 1)))
    w_in = np.ascontiguousarray(np.concatenate([f["L0_attn_W_qkv"], f["L0_attn_W_gate"]]).T)
    experts = f["L0_ffn_weight"][0].transpose(0, 2, 1).reshape(E, PAIRS, 2, C).transpose(0, 2, 1, 3).reshape(E, 2, PAIRS * C)
    ident = np.eye(128, dtype=np.float16)
    sel = np.zeros((128, LOOKS, PAIRS), np.float16)
    for r in range(LOOKS):
        for j in range(2):
            sel[64 * j:64 * j + 64, r, 2 * r + j] = 1
    sums = np.tile(np.eye(PAIRS, dtype=np.float32), (4, 1))
    bit = ((np.arange(PATTERNS)[None, :] >> np.arange(E)[:, None]) & 1).astype(np.float32)
    score = (2 * (2 * bit - 1)).astype(np.float16)
    bias = (-(2 * bit - 1).sum(0) - (E - 1)).reshape(2, 128).T
    given = {
        "x": f["x"].reshape(BC, N), "conv_w": conv, "conv_p": cp, "out_w": ow, "ln_g": f["L0_attn_ln_gamma"],
        "ln_b": f["L0_attn_ln_beta"], "w_in": w_in, "gate_b": f["L0_attn_b_gate"].reshape(HG, 128).T,
        "w_fin": f["L0_attn_W_final"].T.reshape(HG, 128, C).transpose(1, 0, 2), "fin_b": f["L0_attn_b_final"],
        "experts": experts, "proj_w": f["L0_ffn_proj_w"].T, "proj_b": f["L0_ffn_proj_b"].reshape(E, 1),
        "scale": f["L0_ffn_scale"].reshape(C), "c_ident": ident, "c_sel": sel, "c_sum": sums, "c_pat": bit,
        "c_score": score, "c_bias": bias.astype(np.float32),
    }
    nc = bacc.Bacc("TRN2", target_bir_lowering=False, num_devices=1)
    arrays, args = {}, []
    for name in _ORDER:
        v = np.ascontiguousarray(given[name])
        arrays[f"in_{name}"] = v
        args.append(nc.dram_tensor(f"in_{name}", v.shape, mybir.dt.from_np(v.dtype), kind="ExternalInput").ap())
    args.append(nc.dram_tensor("out_0", (B, N, C), F32, kind="ExternalOutput").ap())
    build(nc, *args)
    r = run_bass_kernel_spmd(nc, [arrays], core_ids=[0])
    return r.results[0]["out_0"]
```

```python
from contextlib import ExitStack

import concourse.bass as bass
from concourse import mybir

F32 = mybir.dt.float32
F16 = mybir.dt.float16
ALU = mybir.AluOpType
ACT = mybir.ActivationFunctionType
AX = mybir.AxisListType

B, CH, N = 16, 4, 375
BLOCKS, TAPS = 9, 3
C = 64
HEADS, D = 8, 32
INNER = HEADS * D
TP, TT = 125, 3
TPAD = TP + 1
HG = 2
E, PATTERNS = 8, 256
PAIRS = C // 2
LOOKS = PAIRS // 2
EPS = 1e-5
SCALE = float(D) ** -0.5
BASE = 256.0
ROUND = 1.5 * 2.0 ** 23
BC = B * CH
CUT = 188
FIRST = 3
CHUNKS = 16
GROUPS = HG * TT
BANKS = 3
SLOTS = 3

TENSOR = """
    scores packed attend k0   scores sum q0   scores look0 q1   scores k1 final
    scores gate0 look1 v0 look2 attend look3 gate1 look4   scores look5 look6 attend   scores look7 sgnT
    scores look8 attend v1 look9   scores v2 look10 look11 attend   scores look12 logit
    scores look13 tokT look14 look15   scores attend one0 one1
    """.split()
SCALAR = """
    exp   exp   exp packed   exp k0 sum q0   exp   exp q1   exp k1   exp   exp   exp gate0 v0 sign look2
    exp gate1   exp look6   exp   exp   exp sgnT   exp v1 look9   exp v2   exp   exp   exp look12 logit
    exp   exp   exp tokT bits   exp one0 one1
    """.split()
VECTOR = """
    max   max inverse   max   max gate_old   max   max inverse k0   max   max q0 look0 q1   max k1
    max final inverse look1   max   max variance look3 look4   max   max inverse look5   max
    max look7 look8   max   max inverse gate_new   max look10   max look11   max inverse   max look13
    max look14   max look15
    """.split()
GPSIMD = """
    values values output square values norm values signs next1 values signs next2 signs values signs
    next3 next4
    """.split()
USES = [n for n in TENSOR if n not in ("scores", "attend")]
SHARED = ["look2", "look6", "look9", "look12"]
STAGE = {"tokT": "T", "q0": "P", "q1": "P", "k0": "P", "k1": "P", "gate0": "P", "gate1": "P",
         "v0": "P", "v1": "P", "v2": "P", "final": "F", "sgnT": "F", "logit": "F", "one0": "F", "one1": "F",
         "packed": "Y", "sum": "Y"}
STAGE.update({f"look{i}": "X" for i in range(LOOKS)})
FREED_BY_ACT = {*SHARED, "logit", "tokT", "sum", "packed", "gate0", "gate1", "sgnT", "one0", "one1", "v0", "v1", "v2"}
HALVES = TENSOR.count("scores")
QK = [n for n in USES if n in ("q0", "q1", "k0", "k1")]


def uses_of(stages):
    return [n for n in USES if STAGE[n] in stages]


class Ring:

    def __init__(self, stages, used, by_act, by_dve, phase, before):
        self.names, self.used, self.by_act, self.by_dve, self.phase = uses_of(stages), used, by_act, by_dve, phase
        self.before = before

    def bank(self, name):
        return (self.names.index(name) + self.phase) % BANKS

    def filled(self, name):
        return self.used + self.names.index(name) + 1

    def freed(self, name):
        i = self.names.index(name)
        act = name in FREED_BY_ACT
        n = sum((x in FREED_BY_ACT) == act for x in self.names[:i + 1])
        return (self.by_act if act else self.by_dve) + n

    def freed_before(self, name):
        act = name in FREED_BY_ACT
        n = sum((x in FREED_BY_ACT) == act for x in self.before[self.before.index(name) + 1:])
        return (self.by_act if act else self.by_dve) - n

    def previous(self, name):
        i = self.names.index(name)
        if i >= BANKS:
            p = self.names[i - BANKS]
            return p in FREED_BY_ACT, self.freed(p)
        k = len(self.before) + i - BANKS
        if k < 0:
            return None
        return self.before[k] in FREED_BY_ACT, self.freed_before(self.before[k])


def build(nc, x, conv_w, conv_p, out_w, ln_g, ln_b, w_in, gate_b, w_fin, fin_b, experts, proj_w, proj_b,
          scale, c_ident, c_sel, c_sum, c_pat, c_score, c_bias, out):
    with ExitStack() as ctx:
        def sb(name, shape, dt=F32):
            return ctx.enter_context(nc.sbuf_tensor(name, shape, dt))

        def psum(name, shape, dt=F32):
            return ctx.enter_context(nc.psum_tensor(name, shape, dt))

        def sem(name):
            return ctx.enter_context(nc.semaphore(name))

        scores = psum("scores", [128, 2, 2, 512])
        attend = psum("attend", [128, 512])
        work = psum("work", [128, BANKS, 512])

        cw = sb("cw", [BC, BLOCKS * TAPS, BC])
        cp = sb("cp", [128, 5, BLOCKS])
        bn_s = sb("bn_s", [BC, BLOCKS])
        bn_t = sb("bn_t", [BC, BLOCKS])
        ow = sb("ow", [BC + 1, B * C])
        lng = sb("lng", [TP, C])
        lnb = sb("lnb", [TP, C])
        finb = sb("finb", [TP, C])
        scl = sb("scl", [TP, C])
        w32 = sb("w32", [128, 4 * INNER])
        wh = sb("wh", [128, 4 * INNER], F16)
        wl = sb("wl", [128, 4 * INNER], F16)
        gb = sb("gb", [128, HG])
        gbh = sb("gbh", [128, HG])
        wf = sb("wf", [128, HG, C])
        wfh = sb("wfh", [128, HG, C])
        ex = sb("ex", [CHUNKS * E, 2 * PAIRS * C // CHUNKS])
        pw32 = sb("pw32", [128, E])
        pwh = sb("pwh", [128, E], F16)
        pwl = sb("pwl", [128, E], F16)
        pb = sb("pb", [E, 1])
        ident = sb("ident", [128, 128], F16)
        sel = sb("sel", [128, LOOKS, PAIRS], F16)
        sums = sb("sums", [128, PAIRS])
        pat = sb("pat", [CHUNKS * E, CHUNKS, PATTERNS])
        score = sb("score", [E, PATTERNS], F16)
        sbias = sb("sbias", [128, 2])
        half = sb("half", [128, 48])
        xa = [sb(f"xa{i}", [BC + 1, N]) for i in range(2)]
        xt = sb("xt", [BC, N])
        hr = sb("hr", [BC, N])
        H = sb("H", [TP, B, TT, C])
        cen = sb("cen", [TP, B, TT, C])
        sq = sb("sq", [TP, B, TT, C])
        stat = sb("stat", [TP, 6, B, TT])
        sg = sb("sg", [128, 2, 2, PAIRS * C], F16)
        table = sb("table", [128, 2, PAIRS * C], F16)
        zn = sb("zn", [TP, 2, TT, C])
        tmp = sb("tmp", [TP, TT, C])
        zsp = [sb(f"zsp{i}", [TP, 2, TT, 2, C], F16) for i in range(2)]
        znT = sb("znT", [128, 2, N], F16)
        qk = sb("qk", [128, 4, HG, N], F16)
        stack = [sb(f"stack{i}", [128, 2, 4, HG, N], F16) for i in range(2)]
        vv = [sb(f"vv{i}", [TP, TT, INNER]) for i in range(2)]
        gate = [sb(f"gate{i}", [128, HG, N]) for i in range(2)]
        mx = sb("mx", [TP, SLOTS, 4])
        probs = sb("probs", [TP, SLOTS, 4, N])
        rs = sb("rs", [TP, SLOTS, 4])
        ri = sb("ri", [TP, SLOTS, 4])
        vn = sb("vn", [TP, SLOTS, 4, D])
        att = sb("att", [128, HG, N])
        c3 = sb("c3", [TP, TT, C])
        q3 = sb("q3", [TP, TT, C])
        z3 = sb("z3", [TP, TT, C])
        x3 = [sb(f"x3_{i}", [TP, TT, C]) for i in range(2)]
        st3 = sb("st3", [TP, 5, TT])
        zsg = sb("zsg", [TP, 2, TT, 2, C], F16)
        zxT = [sb(f"zxT{i}", [128, 2, N], F16) for i in range(2)]
        positive = sb("positive", [E, N])
        bits = sb("bits", [E, N], F16)
        onehot = [sb(f"onehot{i}", [128, 2, N], F16) for i in range(2)]
        looked = [pat[:, i, :].bitcast(F16)[:, 0:N] for i in range(len(SHARED))]
        prod = sb("prod", [128, LOOKS, N], F16)
        pk = sb("pk", [128, N])
        psums = sb("psums", [TP, TT, PAIRS])
        dig = sb("dig", [TP, TT, PAIRS])
        num = sb("num", [128, 4])
        yy = sb("yy", [TP, TT, PAIRS, 2])
        yo = sb("yo", [TP, TT, C])

        ld_conv, ld_x, ld_ow, ld_ex, ld_w, ld_c = (sem(n) for n in ("ld_conv", "ld_x", "ld_ow", "ld_ex", "ld_w", "ld_c"))
        ld_conv_rest = sem("ld_conv_rest")
        ld_pat = [sem(f"ld_pat{i}") for i in range(4)]
        consts_set = sem("consts_set")
        ones_set = sem("ones_set")
        bn_ready = sem("bn_ready")
        conv_done = sem("conv_done")
        relu_lo, relu_hi = sem("relu_lo"), sem("relu_hi")
        shifted = sem("shifted")
        x_ready = sem("x_ready")
        h_done = sem("h_done")
        h_copied_v, h_copied_a = sem("h_copied_v"), sem("h_copied_a")
        tab_done = sem("tab_done")
        sg_ready = sem("sg_ready")
        tab_ready = sem("tab_ready")
        w_high, w_ready = sem("w_high"), sem("w_ready")
        ln_v, ln_a, ln_p = sem("ln_v"), sem("ln_a"), sem("ln_p")
        work_full, work_act, work_dve = sem("work_full"), sem("work_act"), sem("work_dve")
        pool_link, zn_ready = sem("pool_link"), sem("zn_ready")
        high_ready, stacked = sem("high_ready"), sem("stacked")
        scored, max_ready, exp_done = sem("scored"), sem("max_ready"), sem("exp_done")
        sum_inverse, v_ready, av_done = sem("sum_inverse"), sem("v_ready"), sem("av_done")
        gated = sem("gated")
        cen_sum, mean_ready, cen_ready, sq_ready, var_ready, norm_link = (
            sem(n) for n in ("cen_sum", "mean_ready", "cen_ready", "sq_ready", "var_ready", "norm_link"))
        split_ready, sign_ready = sem("split_ready"), sem("sign_ready")
        bits_ready, signed = sem("bits_ready"), sem("signed")
        out_link, y_ready, stored = sem("out_link"), sem("y_ready"), sem("stored")

        block = ctx.enter_context(nc.Block())

        STEPS = B + 3
        LOOP0, LOOP1 = 4, 12

        def stages(s):
            on = {"T": 0 <= s + 2 < B, "P": 0 <= s + 1 < B, "F": 0 <= s - 1 < B, "X": 0 <= s - 2 < B, "Y": 0 <= s - 3 < B}
            return "".join(k for k in on if on[k])

        full = uses_of("TPFXY")
        per_act = sum(n in FREED_BY_ACT for n in full)
        per_dve = len(full) - per_act
        assert len(full) % BANKS == 0

        def run_steps(eng, step):
            used = by_act = by_dve = 0
            before = []
            s = -2
            while s < STEPS:
                st = stages(s)
                names = uses_of(st)
                if s == LOOP0:
                    turns = (LOOP1 - LOOP0) // 2
                    with eng.Fori(0, turns) as j:
                        for k in range(2):
                            ring = Ring(st, j * (2 * len(full)) + (used + k * len(full)),
                                        j * (2 * per_act) + (by_act + k * per_act),
                                        j * (2 * per_dve) + (by_dve + k * per_dve),
                                        used % BANKS, before)
                            step(j * 2 + (s + k), (s + k) % 2, st + "A", ring)
                    used, by_act, by_dve = (used + 2 * turns * len(full), by_act + 2 * turns * per_act,
                                            by_dve + 2 * turns * per_dve)
                    s = LOOP1
                else:
                    step(s, s % 2, st + ("A" if 0 <= s < B else ""),
                         Ring(st, used, by_act, by_dve, used % BANKS, before))
                    used += len(names)
                    by_act += sum(n in FREED_BY_ACT for n in names)
                    by_dve += sum(n not in FREED_BY_ACT for n in names)
                    s += 1
                before = names

        def transposed_tiles(bank):
            return work[:, bank, :].bitcast(F16)[:, 0:2 * TT * TPAD].rearrange("p (i n) -> p i n", n=TPAD)[:, :, 0:TP]

        def table_bank(i):
            return attend[:] if i % 2 else scores[:, 1, 1, :]

        PARTS = ((0, FIRST), (FIRST, 9), (9, B))

        def part_bank(i, t):
            lo, hi = PARTS[i]
            n = C * (hi - lo)
            return scores[0:TP, t // 2, t % 2, 0:n] if i == 1 else work[0:TP, t, 0:n]


        def one_b(a, b):
            return a[:, bass.ds(b, 1)] if not isinstance(b, int) else a[:, b:b + 1]

        def at(s, k):
            return isinstance(s, int) and s == k

        def geq(eng, semaphore, count):
            if not isinstance(count, int) or count > 0:
                eng.wait_ge(semaphore, count)

        def normalise(eng, b, par, part):
            def wide(v):
                return v.rearrange("p o t -> p (o t)").unsqueeze(2).to_broadcast([TP, TT, C])

            def rows(v):
                return v[:].unsqueeze(1).to_broadcast([TP, TT, C])

            zt, nt = zn[:, 0], zn[:, 1]
            high = [zsp[par][:, i, :, 0, :] for i in range(2)]
            low = [zsp[par][:, i, :, 1, :] for i in range(2)]
            hb = one_b(H, b).rearrange("p o t c -> p (o t) c")
            k = 9 * b

            def nxt(ins):
                ins.then_inc(pool_link, 1)

            cb, r1b = one_b(cen, b).rearrange("p o t c -> p (o t) c"), wide(one_b(stat[:, 2], b))
            if part == 1:
                geq(eng, pool_link, k)
                geq(eng, zn_ready, b)
                nxt(eng.tensor_tensor(high[0], cb, r1b, ALU.mult))
                nxt(eng.tensor_tensor(zt, cb, r1b, ALU.mult))
            if part == 2:
                eng.wait_ge(pool_link, k + 2)
                nxt(eng.tensor_tensor(tmp[:], zt, wide(one_b(stat[:, 3], b)), ALU.mult))
                eng.wait_ge(pool_link, k + 3)
                nxt(eng.tensor_tensor(nt, tmp[:], rows(lng), ALU.mult))
            if part == 3:
                eng.wait_ge(pool_link, k + 4)
                nxt(eng.tensor_tensor(high[1], nt, rows(lnb), ALU.add))
                nxt(eng.tensor_tensor(tmp[:], zt, rows(finb), ALU.add))
                nxt(eng.tensor_tensor(nt, nt, rows(lnb), ALU.add))
            if part == 4:
                eng.wait_ge(pool_link, k + 7)
                nxt(eng.tensor_tensor(hb, hb, tmp[:], ALU.add))
                nxt(eng.tensor_tensor(low[0], zt, high[0], ALU.subtract))
                eng.tensor_tensor(low[1], nt, high[1], ALU.subtract).then_inc(zn_ready, 1)

        @block.sync
        def _(sp):
            sp.dma_start(xa[0][0:BC, :], x).then_inc(ld_x, 16)
            sp.dma_start(cp[:], conv_p).then_inc(ld_conv, 16)
            sp.dma_start(cw[:, 0:TAPS], conv_w[:, 0:TAPS]).then_inc(ld_conv, 16)
            sp.dma_start(cw[:, TAPS:], conv_w[:, TAPS:]).then_inc(ld_conv_rest, 16)
            sp.dma_start(ex[:], experts).then_inc(ld_ex, 16)
            for i in range(4):
                sp.dma_start(pat[:, 4 * i:4 * i + 4], c_pat[:, 4 * i:4 * i + 4]).then_inc(ld_pat[i], 16)
                if i == 0:
                    for r in range(2):
                        sp.dma_start(w32[C * r:C * r + C, :], w_in).then_inc(ld_w, 16)
            sp.dma_start(ow[:], out_w).then_inc(ld_ow, 16)
            for r in range(2):
                sp.dma_start(pw32[C * r:C * r + C, :], proj_w).then_inc(ld_w, 16)
            sp.dma_start(wf[:], w_fin).then_inc(ld_w, 16)
            sp.dma_start(gb[:], gate_b).then_inc(ld_w, 16)
            for dst, src in ((ident, c_ident), (sel, c_sel), (sums, c_sum), (score, c_score), (sbias, c_bias),
                             (pb, proj_b)):
                sp.dma_start(dst[:], src).then_inc(ld_c, 16)
            for dst, src in ((lng, ln_g), (lnb, ln_b), (finb, fin_b), (scl, scale)):
                sp.dma_start(dst[:], src.partition_broadcast(TP)).then_inc(ld_c, 16)

            def step(s, par, st, ring):
                if "Y" in st:
                    dst = out[s - 3:s - 2] if isinstance(s, int) else out[bass.ds(sp.snap(s - 3), 1)]
                    sp.wait_ge(y_ready, s - 3 + 1)
                    sp.dma_start(dst.rearrange("o (p t) c -> (o p) t c", t=TT), yo[:]).then_inc(stored, 16)
                if "P" in st:
                    b = s + 1
                    sp.wait_ge(work_dve, ring.freed(QK[-1]))
                    geq(sp, stacked, 256 * b)
                    for r in range(4):
                        qi, ki = r // 2, 2 + r % 2
                        for h in range(4):
                            sp.dma_start(stack[1 - par][D * r:D * r + D, :, h, :, :],
                                         qk[D * h:D * h + D, qi:ki + 1:ki - qi, :, :]).then_inc(stacked, 16)

            run_steps(sp, step)
            sp.wait_ge(stored, 16 * B)

        @block.tensor
        def _(pe):
            def table_mm(i):
                k, hp, q = i // 2, i // CHUNKS, i % CHUNKS
                if i == 0:
                    pe.wait_ge(ld_ex, 16)
                if hp == 0 and q % 4 == 0:
                    pe.wait_ge(ld_pat[q // 4], 16)
                if i % 2 == 0 and k >= 2:
                    pe.wait_ge(sg_ready, k - 1)
                c = 256 * (i % 2)
                pe.matmul(table_bank(k)[:, c:c + 256], pat[:, q, 128 * hp:128 * hp + 128], ex[:],
                          start=True, stop=True).then_inc(tab_done, 1)

            pe.wait_ge(ld_conv, 32)
            pe.wait_ge(ld_x, 16)
            for n in range(BLOCKS):
                d = 2 ** n
                geq(pe, x_ready, n)
                if n == 1:
                    pe.wait_ge(ld_conv_rest, 16)
                cur = xa[n % 2]
                cuts = ((0, CUT), (CUT, N))
                spans = [[(k, max(lo, (2 - k) * d), hi) for k in (2, 1, 0) if max(lo, (2 - k) * d) < hi] for lo, hi in cuts]
                for t in range(TAPS):
                    for c in range(2):
                        if t >= len(spans[c]):
                            continue
                        k, lo, hi = spans[c][t]
                        sh = (2 - k) * d
                        mm = pe.matmul(scores[BC * c:BC * c + BC, n % 2, 0, lo - cuts[c][0]:hi - cuts[c][0]],
                                       cw[:, n * TAPS + k, :], cur[0:BC, lo - sh:hi - sh],
                                       start=(t == 0), stop=(t == len(spans[c]) - 1), skip_group_check=True)
                mm.then_inc(conv_done, 1)
                for i in range(2):
                    table_mm(2 * n + i)
            pe.wait_ge(x_ready, BLOCKS)
            pe.wait_ge(ones_set, 2)
            pe.wait_ge(ld_ow, 16)
            for i, (lo, hi) in enumerate(PARTS):
                for t in range(TT):
                    if i == 2 and t == 0:
                        pe.wait_ge(h_copied_v, 1)
                    mm = pe.matmul(part_bank(i, t), xa[BLOCKS % 2][:, t:N:TT], ow[:, C * lo:C * hi], start=True, stop=True)
                    if i > 0 or t == TT - 1:
                        mm.then_inc(h_done, 1)
            for i in range(2 * BLOCKS, 2 * CHUNKS):
                table_mm(i)
            pe.wait_ge(sg_ready, 16)
            pe.wait_ge(w_ready, 5)
            pe.wait_ge(ld_c, 160)
            pe.wait_ge(h_copied_a, 2 * TT)

            def step(s, par, st, ring):
                nxt = 1 - par

                def open_bank(name):
                    prev = ring.previous(name)
                    if prev:
                        pe.wait_ge(work_act if prev[0] else work_dve, prev[1])
                    return work[:, ring.bank(name), :]

                def tokT():
                    pe.wait_ge(zn_ready, s + 3)
                    o = open_bank("tokT").bitcast(F16)
                    for i in range(2):
                        for t in range(TT):
                            mm = pe.transpose(o[:, TPAD * (TT * i + t):TPAD * (TT * i + t) + TP],
                                              zsp[par][:, i, t, :, :].rearrange("p a c -> p (a c)"), ident[0:TP, 0:TP])
                    mm.then_inc(work_full, 1)

                def feature_major(name, col, src):
                    if name == QK[0]:
                        pe.wait_ge(work_act, ring.freed_before("tokT"))
                    o = open_bank(name)
                    pe.matmul(o[:, 0:N], wh[:, col:col + 128], znT[:, src, :], start=True, stop=False)
                    pe.matmul(o[:, 0:N], wl[:, col:col + 128], znT[:, src, :], start=False, stop=True).then_inc(work_full, 1)

                def token_major(t):
                    o = open_bank(f"v{t}")
                    for w in (wh, wl):
                        mm = pe.matmul(o[0:TP, 0:INNER], znT[:, 1, TP * t:TP * t + TP], w[:, 2 * INNER:3 * INNER],
                                       start=(w is wh), stop=(w is wl))
                    mm.then_inc(work_full, 1)

                def final():
                    pe.wait_ge(gated, 2 * (s - 1) + 2)
                    o = open_bank("final")
                    for t in range(TT):
                        for g in range(HG):
                            mm = pe.matmul(o[0:TP, C * t:C * t + C], att[:, g, TP * t:TP * t + TP], wfh[:, g, :],
                                           start=(g == 0), stop=(g == HG - 1))
                    mm.then_inc(work_full, 1)

                def sgnT():
                    pe.wait_ge(split_ready, s)
                    pe.wait_ge(sign_ready, s)
                    o = open_bank("sgnT").bitcast(F16)
                    for i in range(2):
                        for t in range(TT):
                            mm = pe.transpose(o[:, TPAD * (TT * i + t):TPAD * (TT * i + t) + TP],
                                              zsg[:, i, t, :, :].rearrange("p a c -> p (a c)"), ident[0:TP, 0:TP])
                    mm.then_inc(work_full, 1)

                def logit():
                    pe.wait_ge(work_act, ring.freed("sgnT"))
                    o = open_bank("logit")
                    pe.matmul(o[0:E, 0:N], pwh[:], zxT[nxt][:, 0, :], start=True, stop=False)
                    pe.matmul(o[0:E, 0:N], pwl[:], zxT[nxt][:, 0, :], start=False, stop=True).then_inc(work_full, 1)

                def one(i):
                    if i == 0:
                        pe.wait_ge(bits_ready, s)
                    o = open_bank(f"one{i}")
                    pe.matmul(o[:, 0:N], score[:, 128 * i:128 * i + 128], bits[:], start=True,
                              stop=True).then_inc(work_full, 1)

                def look(r):
                    if r == 0:
                        pe.wait_ge(work_act, ring.freed_before("one1"))
                        if at(s, 2):
                            pe.wait_ge(tab_ready, 4)
                    o = open_bank(f"look{r}")
                    pe.matmul(o[:, 0:N], table[:, 0, 128 * r:128 * r + 128], onehot[par][:, 0, :], start=True, stop=False)
                    pe.matmul(o[:, 0:N], table[:, 1, 128 * r:128 * r + 128], onehot[par][:, 1, :], start=False,
                              stop=True).then_inc(work_full, 1)

                def reduce():
                    o = open_bank("packed")
                    pe.wait_ge(work_dve, ring.freed_before(f"look{LOOKS - 1}"))
                    pe.wait_ge(signed, len(SHARED) * (s - 2))
                    for r in range(LOOKS):
                        c = r % 4
                        mm = pe.matmul(o[32 * c:32 * c + 32, 0:N], sel[:, r, :], prod[:, r, :], start=(r < 4),
                                       stop=(r >= LOOKS - 4), skip_group_check=True)
                    mm.then_inc(work_full, 1)

                def total():
                    pe.wait_ge(work_act, ring.freed("packed"))
                    o = open_bank("sum")
                    for t in range(TT):
                        mm = pe.matmul(o[0:TP, PAIRS * t:PAIRS * t + PAIRS], pk[:, TP * t:TP * t + TP], sums[:],
                                       start=True, stop=True)
                    mm.then_inc(work_full, 1)

                def sum_queries(b, g):
                    pe.wait_ge(v_ready, 6 * b + g + 1)
                    if g % TT == 0:
                        geq(pe, gated, 2 * b + g // TT)
                    for h in range(4):
                        mm = pe.matmul(attend[32 * h:32 * h + 32, 0:N], vn[:, g % SLOTS, h, :], probs[:, g % SLOTS, h, :],
                                       start=(g % TT == 0), stop=(g % TT == TT - 1), skip_group_check=True)
                    mm.then_inc(av_done, 1)

                todo = {"tokT": tokT, "q0": lambda: feature_major("q0", 0, 1), "q1": lambda: feature_major("q1", 128, 1),
                        "k0": lambda: feature_major("k0", INNER, 1), "k1": lambda: feature_major("k1", INNER + 128, 1),
                        "gate0": lambda: feature_major("gate0", 3 * INNER, 0),
                        "gate1": lambda: feature_major("gate1", 3 * INNER + 128, 0),
                        "v0": lambda: token_major(0), "v1": lambda: token_major(1), "v2": lambda: token_major(2),
                        "final": final, "sgnT": sgnT, "logit": logit, "one0": lambda: one(0), "one1": lambda: one(1),
                        "packed": reduce, "sum": total}
                for r in range(LOOKS):
                    todo[f"look{r}"] = lambda r=r: look(r)

                def scores_of(b, h, slots):
                    hg, t, p = h // 2 // TT, h // 2 % TT, h % 2
                    for i in range(2):
                        geq(pe, exp_done, 2 * (12 * b + h) - 3 + i)
                        pe.matmul(scores[0:TP, p, i, 0:N], slots[:, 0, 2 * p + i, hg, TP * t:TP * t + TP],
                                  slots[:, 1, 2 * p + i, hg, :], start=True, stop=True).then_inc(scored, 1)

                h = g = 0
                for name in TENSOR:
                    if name == "scores":
                        h += 1
                        if h < HALVES and "A" in st:
                            scores_of(s, h, stack[par])
                        if h == HALVES and "P" in st:
                            pe.wait_ge(stacked, 256 * (s + 2))
                            scores_of(s + 1, 0, stack[nxt])
                    elif name == "attend":
                        if g == 0 and "F" in st:
                            sum_queries(s - 1, GROUPS - 1)
                        if g > 0 and "A" in st:
                            sum_queries(s, g - 1)
                        g += 1
                    elif STAGE[name] in st:
                        todo[name]()

            run_steps(pe, step)

        @block.scalar
        def _(act):
            def table_sign(i):
                act.wait_ge(tab_done, 2 * i + 2)
                hp, dg, ch = i // 8, i // 4 % 2, i % 4
                act.activation(sg[:, hp, dg, 512 * ch:512 * ch + 512], table_bank(i),
                               ACT.Sign).then_inc(sg_ready, 1)

            act.wait_ge(consts_set, 1)
            act.activation(q3[0:1, 0, 0:1], half[0:1, 0:1], ACT.Relu)
            act.wait_ge(ld_conv, 32)
            for n in range(BLOCKS):
                act.wait_ge(conv_done, n + 1)
                act.activation(hr[:, CUT:N], scores[BC:2 * BC, n % 2, 0, 0:N - CUT], ACT.Relu,
                               bias=cp[BC:2 * BC, 0, n:n + 1]).then_inc(relu_hi, 1)
                table_sign(n)
                if n == 4:
                    act.wait_ge(ld_w, 96)
                    act.activation(wh[:], w32[:], ACT.Copy).then_inc(w_high, 1)
            for i in (1, 2):
                lo, hi = PARTS[i]
                for t in range(TT):
                    act.wait_ge(h_done, TT * (i - 1) + t + 2)
                    act.activation(H[:, lo:hi, t, :], part_bank(i, t).rearrange("p (b c) -> p b c", c=C),
                                   ACT.Copy).then_inc(h_copied_a, 1)
            for i in range(BLOCKS, 16):
                table_sign(i)

            def square_others():
                act.wait_ge(ln_v, 6)
                act.activation(sq[:, FIRST:].rearrange("p b t c -> p (b t c)"),
                               cen[:, FIRST:].rearrange("p b t c -> p (b t c)"), ACT.Square).then_inc(ln_a, 1)

            def step(s, par, st, ring):
                nxt = 1 - par

                def high(i):
                    name = ("q0", "q1", "k0", "k1")[i]
                    if name == QK[0]:
                        geq(act, stacked, 256 * (s + 1))
                    act.wait_ge(work_full, ring.filled(name))
                    act.activation(qk[:, 2 * (i // 2), i % 2, :], work[:, ring.bank(name), 0:N], ACT.Copy,
                                   scale=(-SCALE if i < 2 else 1.0)).then_inc(high_ready, 1)

                def gates(i):
                    name = f"gate{i}"
                    if i == 0:
                        geq(act, gated, 2 * s)
                    act.wait_ge(work_full, ring.filled(name))
                    act.activation(gate[nxt][:, i, :], work[:, ring.bank(name), 0:N], ACT.Tanh, bias=gbh[:, i:i + 1],
                                   scale=0.5).then_inc(work_act, 1)

                def values(t):
                    if t == 0:
                        geq(act, v_ready, 6 * s)
                    act.wait_ge(work_full, ring.filled(f"v{t}"))
                    act.activation(vv[nxt][:, t, :], work[0:TP, ring.bank(f"v{t}"), 0:INNER],
                                   ACT.Copy).then_inc(work_act, 1)

                def sign():
                    act.wait_ge(cen_ready, s)
                    for r in range(2):
                        a = act.activation(zsg[:, 1, :, r, :], c3[:], ACT.Sign)
                    a.then_inc(sign_ready, 1)

                def transposed():
                    act.wait_ge(work_full, ring.filled("sgnT"))
                    act.activation(zxT[nxt][:].rearrange("p a (t n) -> p (a t) n", t=TT),
                                   transposed_tiles(ring.bank("sgnT")), ACT.Copy).then_inc(work_act, 1)

                def one(i):
                    name = f"one{i}"
                    act.wait_ge(work_full, ring.filled(name))
                    act.activation(onehot[nxt][:, i, :], work[:, ring.bank(name), 0:N], ACT.Relu,
                                   bias=sbias[:, i:i + 1]).then_inc(work_act, 1)

                def logit():
                    act.wait_ge(work_full, ring.filled("logit"))
                    act.activation(positive[:], work[0:E, ring.bank("logit"), 0:N], ACT.Relu,
                                   bias=pb[:]).then_inc(work_act, 1)

                def set_bits():
                    act.wait_ge(work_act, ring.freed("logit"))
                    act.activation(bits[:], positive[:], ACT.Sign).then_inc(bits_ready, 1)

                def copy_look(i):
                    act.wait_ge(work_full, ring.filled(SHARED[i]))
                    geq(act, signed, len(SHARED) * (s - 3) + i + 1)
                    act.activation(looked[i], work[:, ring.bank(SHARED[i]), 0:N], ACT.Copy).then_inc(work_act, 1)

                def copy_packed():
                    act.wait_ge(work_full, ring.filled("packed"))
                    act.activation(pk[:], work[:, ring.bank("packed"), 0:N], ACT.Copy).then_inc(work_act, 1)

                def tokT():
                    act.wait_ge(work_full, ring.filled("tokT"))
                    act.activation(znT[:].rearrange("p a (t n) -> p (a t) n", t=TT),
                                   transposed_tiles(ring.bank("tokT")), ACT.Copy).then_inc(work_act, 1)

                def copy_sums():
                    act.wait_ge(work_full, ring.filled("sum"))
                    geq(act, y_ready, s - 3)
                    act.activation(psums[:].rearrange("p t c -> p (t c)"), work[0:TP, ring.bank("sum"), 0:TT * PAIRS],
                                   ACT.Copy).then_inc(work_act, 1)

                todo = {"tokT": tokT, "sum": copy_sums, "q0": lambda: high(0), "q1": lambda: high(1), "k0": lambda: high(2), "k1": lambda: high(3),
                        "gate0": lambda: gates(0), "gate1": lambda: gates(1), "v0": lambda: values(0),
                        "v1": lambda: values(1), "v2": lambda: values(2), "sgnT": transposed, "one0": lambda: one(0),
                        "one1": lambda: one(1), "packed": copy_packed, "logit": logit,
                        **{n: lambda i=i: copy_look(i) for i, n in enumerate(SHARED)}}

                def exponential(k):
                    h, g, i = k // 2, k // 4, k % 4
                    act.wait_ge(max_ready, 24 * s + k + 1)
                    if i == 0:
                        geq(act, av_done, 6 * s + g - SLOTS + 1)
                    act.activation(probs[:, g % SLOTS, i, :], scores[0:TP, h % 2, i % 2, 0:N], ACT.Exp, scale=-1.0,
                                   bias=mx[:, g % SLOTS, i:i + 1],
                                   accum_out=rs[:, g % SLOTS, i:i + 1]).then_inc(exp_done, 1)

                k = 0
                for name in SCALAR:
                    if name == "exp":
                        if "A" in st:
                            exponential(k)
                        k += 1
                    elif name == "sign":
                        if "F" in st:
                            sign()
                    elif name == "bits":
                        if "F" in st:
                            set_bits()
                    elif STAGE[name] in st:
                        if name == "tokT" and at(s, -1):
                            square_others()
                        todo[name]()

            run_steps(act, step)

        @block.vector
        def _(dve):
            for i in range(2):
                dve.memset(xa[i][BC:BC + 1, :], 1.0).then_inc(ones_set, 1)
            dve.wait_ge(ld_conv, 32)
            for n in range(BLOCKS):
                cur, new = xa[n % 2], xa[(n + 1) % 2]
                dve.wait_ge(conv_done, n + 1)
                dve.tensor_scalar(hr[:, 0:CUT], scores[0:BC, n % 2, 0, 0:CUT], cp[0:BC, 0, n:n + 1], 0.0,
                                  ALU.add, ALU.max).then_inc(relu_lo, 1)
                dve.wait_ge(relu_lo, n + 1)
                dve.wait_ge(relu_hi, n + 1)
                dve.wait_ge(shifted, n + 1)
                dve.scalar_tensor_tensor(new[0:BC, :], hr[:], bn_s[:, n:n + 1], xt[:], ALU.mult, ALU.add).then_inc(x_ready, 1)
                if n == 4:
                    dve.wait_ge(w_high, 1)
                    dve.tensor_tensor(wl[:], w32[:], wh[:], ALU.subtract).then_inc(w_ready, 1)
                if n == 5:
                    dve.tensor_copy(pwh[:], pw32[:]).then_inc(w_ready, 1)
                    dve.wait_ge(w_ready, 2)
                    dve.tensor_tensor(pwl[:], pw32[:], pwh[:], ALU.subtract).then_inc(w_ready, 1)
                if n == 6:
                    dve.tensor_scalar(gbh[:], gb[:], 0.5, None, ALU.mult).then_inc(w_ready, 1)
                    dve.tensor_scalar(wfh[:], wf[:], 0.5, None, ALU.mult).then_inc(w_ready, 1)
            s1, v1 = stat[:, 0], stat[:, 1]
            lo, hi = PARTS[0]
            dve.wait_ge(h_done, 1)
            dve.tensor_copy(H[:, lo:hi].rearrange("p b t c -> p t b c"),
                            work[0:TP, 0:TT, 0:C * (hi - lo)].rearrange("p t (b c) -> p t b c", c=C)).then_inc(h_copied_v, 1)
            dve.wait_ge(h_copied_v, 1)

            def add_features(lo, hi):
                dve.tensor_reduce(s1[:, lo:hi], H[:, lo:hi], AX.X, ALU.add).then_inc(ln_v, 1)

            def centre(lo, hi, k):
                n = TT * (hi - lo)
                dve.wait_ge(ln_v, k + 1)
                dve.scalar_tensor_tensor(cen[:, lo:hi].rearrange("p b t c -> p (b t) c"),
                                         s1[:, lo:hi].rearrange("p b t -> p (b t)").unsqueeze(2).to_broadcast([TP, n, C]), -1.0 / C,
                                         H[:, lo:hi].rearrange("p b t c -> p (b t) c"), ALU.mult, ALU.add).then_inc(ln_v, 1)

            add_features(lo, hi)
            centre(lo, hi, 0)
            dve.wait_ge(ln_v, 2)
            dve.tensor_tensor(sq[:, lo:hi], cen[:, lo:hi], cen[:, lo:hi], ALU.mult).then_inc(ln_v, 1)
            dve.wait_ge(ln_v, 3)
            dve.tensor_reduce(v1[:, lo:hi], sq[:, lo:hi], AX.X, ALU.add).then_inc(ln_v, 1)
            dve.wait_ge(ld_c, 160)
            dve.wait_ge(ln_p, 6)
            for part in range(1, 5):
                normalise(dve, 0, 0, part)
            dve.wait_ge(h_copied_a, 2 * TT)
            add_features(FIRST, B)

            def table_part(i):
                if i == 0:
                    dve.wait_ge(sg_ready, 16)
                hp, c = i // 2, i % 2 * (PAIRS * C // 2)
                dve.scalar_tensor_tensor(table[:, hp, c:c + PAIRS * C // 2], sg[:, hp, 1, c:c + PAIRS * C // 2], BASE,
                                         sg[:, hp, 0, c:c + PAIRS * C // 2], ALU.mult, ALU.add).then_inc(tab_ready, 1)

            def step(s, par, st, ring):
                nxt = 1 - par

                def low(i):
                    name = ("q0", "q1", "k0", "k1")[i]
                    dve.wait_ge(high_ready, 4 * (s + 1) + QK.index(name) + 1)
                    dve.scalar_tensor_tensor(qk[:, 2 * (i // 2) + 1, i % 2, :], work[:, ring.bank(name), 0:N],
                                             (-SCALE if i < 2 else 1.0), qk[:, 2 * (i // 2), i % 2, :], ALU.mult,
                                             ALU.subtract).then_inc(work_dve, 1)

                def final():
                    dve.wait_ge(work_full, ring.filled("final"))
                    if "Y" in st or "X" in st:
                        geq(dve, y_ready, s - 2)
                    hz = one_b(H, s - 1).rearrange("p o t c -> p (o t c)")
                    dve.tensor_tensor(x3[nxt][:].rearrange("p t c -> p (t c)"), work[0:TP, ring.bank("final"), 0:TT * C], hz,
                                      ALU.add).then_inc(work_dve, 1)
                    dve.wait_ge(work_dve, ring.freed("final"))
                    dve.tensor_reduce(st3[:, 0], x3[nxt][:], AX.X, ALU.add).then_inc(cen_sum, 1)

                def variance():
                    dve.wait_ge(sq_ready, s)
                    dve.tensor_reduce(st3[:, 1], q3[:], AX.X, ALU.add).then_inc(var_ready, 1)
                    dve.wait_ge(var_ready, 2 * (s - 1) + 1)
                    dve.tensor_scalar(st3[:, 2], st3[:, 1], 1.0 / C, EPS, ALU.mult, ALU.add).then_inc(var_ready, 1)

                def look(r):
                    name = f"look{r}"
                    dve.wait_ge(work_full, ring.filled(name))
                    dve.tensor_tensor(prod[:, r, :], work[:, ring.bank(name), 0:N], zxT[par][:, 1, :],
                                      ALU.mult).then_inc(work_dve, 1)

                todo = {"q0": lambda: low(0), "q1": lambda: low(1), "k0": lambda: low(2),
                        "k1": lambda: low(3), "final": final}
                for r in range(LOOKS):
                    todo[f"look{r}"] = lambda r=r: look(r)

                def inverse(b, g):
                    dve.wait_ge(exp_done, 24 * b + 4 * g + 4)
                    dve.reciprocal(ri[:, g % SLOTS, :], rs[:, g % SLOTS, :]).then_inc(sum_inverse, 1)

                def apply_gate(b, hg, which):
                    dve.wait_ge(av_done, 6 * b + TT * hg + TT)
                    dve.scalar_tensor_tensor(att[:, hg, :], gate[which][:, hg, :], 1.0, attend[:, 0:N], ALU.add,
                                             ALU.mult).then_inc(gated, 1)

                k = g = 0
                for name in VECTOR:
                    if name == "max":
                        if "A" in st:
                            dve.wait_ge(scored, 24 * s + k + 1)
                            dve.tensor_reduce(mx[:, k // 4 % SLOTS, k % 4:k % 4 + 1], scores[0:TP, k // 2 % 2, k % 2, 0:N],
                                              AX.X, ALU.min).then_inc(max_ready, 1)
                        if at(s, 0) and k in (4, 6, 8, 10):
                            table_part(k // 2 - 2)
                        k += 1
                    elif name == "inverse":
                        if g == 0 and "F" in st:
                            inverse(s - 1, GROUPS - 1)
                        if g > 0 and "A" in st:
                            inverse(s, g - 1)
                        g += 1
                    elif name == "gate_old":
                        if "F" in st:
                            apply_gate(s - 1, 1, nxt)
                    elif name == "gate_new":
                        if "A" in st:
                            apply_gate(s, 0, par)
                    elif name == "variance":
                        if "F" in st:
                            variance()
                    elif STAGE[name] in st:
                        todo[name]()
                if at(s, -1):
                    centre(FIRST, B, 4)
                    dve.wait_ge(ln_a, 1)
                    dve.tensor_reduce(v1[:, FIRST:], sq[:, FIRST:], AX.X, ALU.add).then_inc(ln_v, 1)

            run_steps(dve, step)

        @block.gpsimd
        def _(pool):
            pool.memset(half[:], -0.5).then_inc(consts_set, 1)
            for i, v in enumerate((1.0 / BASE, ROUND, BASE, 1.0 / C)):
                pool.memset(num[:, i:i + 1], v).then_inc(consts_set, 1)
            pool.wait_ge(consts_set, 5)
            pool.wait_ge(ld_conv, 32)
            pool.tensor_scalar(bn_s[:], cp[0:BC, 4, :], EPS, None, ALU.add).then_inc(bn_ready, 1)
            pool.wait_ge(bn_ready, 1)
            pool.tensor_tensor(bn_t[:], bn_s[:], half[0:BC, 0:BLOCKS], ALU.pow).then_inc(bn_ready, 1)
            pool.wait_ge(bn_ready, 2)
            pool.tensor_tensor(bn_s[:], bn_t[:], cp[0:BC, 1, :], ALU.mult).then_inc(bn_ready, 1)
            pool.wait_ge(bn_ready, 3)
            pool.tensor_tensor(bn_t[:], bn_s[:], cp[0:BC, 3, :], ALU.mult).then_inc(bn_ready, 1)
            pool.wait_ge(bn_ready, 4)
            pool.tensor_tensor(bn_t[:], cp[0:BC, 2, :], bn_t[:], ALU.subtract).then_inc(bn_ready, 1)
            pool.wait_ge(bn_ready, 5)
            pool.wait_ge(ld_x, 16)
            for n in range(BLOCKS):
                geq(pool, x_ready, n)
                pool.tensor_scalar(xt[:], xa[n % 2][0:BC, :], bn_t[:, n:n + 1], None, ALU.add).then_inc(shifted, 1)

            def deviations(lo, hi, k):
                n = TT * (hi - lo)
                v1, r1, r2, t1, t2 = (stat[:, i, lo:hi].rearrange("p b t -> p (b t)") for i in range(1, 6))
                hv = half[0:TP, 0:n]
                for i, (o, a, b, op) in enumerate(((t1, v1, None, None), (r1, t1, hv, ALU.pow), (t2, r1, r1, ALU.mult),
                                                   (t1, t2, v1, ALU.mult), (t2, t1, None, None), (r2, t2, hv, ALU.pow))):
                    if b is None:
                        ins = pool.tensor_scalar(o, a, 1.0 / C, EPS, ALU.mult, ALU.add)
                    else:
                        ins = pool.tensor_tensor(o, a, b, op)
                    ins.then_inc(ln_p, 1)
                    pool.wait_ge(ln_p, k + i + 1)

            pool.wait_ge(ln_v, 4)
            deviations(0, 1, 0)
            deviations(1, FIRST, 6)
            pool.wait_ge(ld_c, 160)

            def step(s, par, st, ring):
                nxt = 1 - par

                def scale_values(b, g, which):
                    pool.wait_ge(sum_inverse, 6 * b + g + 1)
                    geq(pool, av_done, 6 * b + g - SLOTS + 1)
                    hg, t = g // TT, g % TT
                    pool.tensor_tensor(vn[:, g % SLOTS], vv[which][:, t, 128 * hg:128 * hg + 128].rearrange("p (h d) -> p h d", d=D),
                                       ri[:, g % SLOTS, :].unsqueeze(2).to_broadcast([TP, 4, D]), ALU.mult).then_inc(v_ready, 1)

                def square():
                    pool.wait_ge(cen_sum, s)
                    pool.tensor_tensor(st3[:, 4], st3[:, 0], num[0:TP, 3:4].to_broadcast([TP, TT]), ALU.mult).then_inc(mean_ready, 1)
                    pool.wait_ge(mean_ready, s)
                    pool.tensor_tensor(c3[:], x3[nxt][:],
                                       st3[:, 4].unsqueeze(2).to_broadcast([TP, TT, C]), ALU.subtract).then_inc(cen_ready, 1)
                    pool.wait_ge(cen_ready, s)
                    pool.tensor_tensor(q3[:], c3[:], c3[:], ALU.mult).then_inc(sq_ready, 1)

                def norm3():
                    k = 3 * (s - 1)
                    pool.wait_ge(var_ready, 2 * s)
                    geq(pool, split_ready, s - 1)
                    pool.tensor_tensor(st3[:, 3], st3[:, 2], half[0:TP, 0:TT], ALU.pow).then_inc(norm_link, 1)
                    pool.wait_ge(norm_link, k + 1)
                    wide = st3[:, 3].unsqueeze(2).to_broadcast([TP, TT, C])
                    pool.tensor_tensor(zsg[:, 0, :, 0, :], c3[:], wide, ALU.mult).then_inc(norm_link, 1)
                    pool.tensor_tensor(z3[:], c3[:], wide, ALU.mult).then_inc(norm_link, 1)
                    pool.wait_ge(norm_link, k + 3)
                    pool.tensor_tensor(zsg[:, 0, :, 1, :], z3[:], zsg[:, 0, :, 0, :], ALU.subtract).then_inc(split_ready, 1)

                def apply_signs(i):
                    pool.wait_ge(work_act, ring.freed(SHARED[i]))
                    r = int(SHARED[i][4:])
                    pool.tensor_tensor(prod[:, r, :], looked[i], zxT[par][:, 1, :], ALU.mult).then_inc(signed, 1)

                def output():
                    pool.wait_ge(work_act, ring.freed("sum"))
                    geq(pool, stored, 16 * (s - 3))

                    def number(i):
                        return num[0:TP, i:i + 1].unsqueeze(1).to_broadcast([TP, TT, PAIRS])

                    k = 6 * (s - 3)
                    even, odd = yy[:, :, :, 0], yy[:, :, :, 1]
                    y3 = yy[:].rearrange("p t c g -> p t (c g)")
                    for i, (o, a, b, op) in enumerate((
                            (dig[:], psums[:], number(0), ALU.mult), (dig[:], dig[:], number(1), ALU.add),
                            (odd, dig[:], number(1), ALU.subtract), (dig[:], odd, number(2), ALU.mult),
                            (even, psums[:], dig[:], ALU.subtract),
                            (yo[:], y3, scl[:].unsqueeze(1).to_broadcast([TP, TT, C]), ALU.mult))):
                        pool.tensor_tensor(o, a, b, op).then_inc(out_link, 1)
                        pool.wait_ge(out_link, k + i + 1)
                    pool.tensor_tensor(yo[:], yo[:], x3[nxt][:],
                                       ALU.add).then_inc(y_ready, 1)

                g = i = 0
                for name in GPSIMD:
                    if name == "values":
                        if g == 0 and "F" in st:
                            scale_values(s - 1, GROUPS - 1, nxt)
                        if g > 0 and "A" in st:
                            scale_values(s, g - 1, par)
                        g += 1
                    elif name == "signs":
                        if "X" in st:
                            apply_signs(i)
                        i += 1
                    elif name == "output":
                        if "Y" in st:
                            output()
                    elif name == "square":
                        if "F" in st:
                            square()
                    elif name == "norm":
                        if "F" in st:
                            norm3()
                    elif not isinstance(s, int) or 0 < s + 3 < B:
                        if name == "next1" and not at(s, -2):
                            pool.wait_ge(work_act, ring.freed_before("tokT"))
                        normalise(pool, s + 3, nxt, int(name[-1]))
                if at(s, -1):
                    pool.wait_ge(ln_v, 7)
                    deviations(FIRST, B, 12)

            run_steps(pool, step)


_ORDER = ["x", "conv_w", "conv_p", "out_w", "ln_g", "ln_b", "w_in", "gate_b", "w_fin", "fin_b", "experts",
          "proj_w", "proj_b", "scale", "c_ident", "c_sel", "c_sum", "c_pat", "c_score", "c_bias"]


def kernel(**a):
    import numpy as np
    import concourse.bacc as bacc
    from concourse.bass_utils import run_bass_kernel_spmd

    f = {k: np.ascontiguousarray(v) for k, v in a.items()}
    z = lambda *s: np.zeros(s, np.float32)
    conv = z(BC, BLOCKS * TAPS, BC)
    ow = z(BC + 1, B * C)
    cwt = f["L0_tok_conv_w"].transpose(2, 0, 3, 1).reshape(CH, BLOCKS * TAPS, CH)
    for b in range(B):
        conv[CH * b:CH * b + CH, :, CH * b:CH * b + CH] = cwt
        ow[CH * b:CH * b + CH, C * b:C * b + C] = f["L0_tok_out_w"][:, :, 0].T
        ow[BC, C * b:C * b + C] = f["L0_tok_out_b"]
    par = np.stack([f["L0_tok_conv_b"], f["L0_tok_bn_gamma"], f["L0_tok_bn_beta"], f["L0_tok_bn_mean"],
                    f["L0_tok_bn_var"]])
    cp = np.ascontiguousarray(np.tile(par.transpose(2, 0, 1), (2 * B, 1, 1)))
    w_in = np.ascontiguousarray(np.concatenate([f["L0_attn_W_qkv"], f["L0_attn_W_gate"]]).T)
    experts = f["L0_ffn_weight"][0].transpose(0, 2, 1).reshape(E, PAIRS, 2, C).transpose(0, 2, 1, 3).reshape(E, CHUNKS, 256)
    experts = experts.transpose(1, 0, 2).reshape(CHUNKS * E, 256)
    ident = np.eye(128, dtype=np.float16)
    sel = np.zeros((128, LOOKS, PAIRS), np.float16)
    for r in range(LOOKS):
        for j in range(2):
            sel[64 * j:64 * j + 64, r, 2 * r + j] = 1
    sums = np.tile(np.eye(PAIRS, dtype=np.float32), (4, 1))
    bit = ((np.arange(PATTERNS)[None, :] >> np.arange(E)[:, None]) & 1).astype(np.float32)
    pat = np.zeros((CHUNKS, E, CHUNKS, PATTERNS), np.float32)
    for q in range(CHUNKS):
        pat[q, :, q] = bit
    pat = pat.reshape(CHUNKS * E, CHUNKS, PATTERNS)
    score = (2 * (2 * bit - 1)).astype(np.float16)
    bias = (-(2 * bit - 1).sum(0) - (E - 1)).reshape(2, 128).T
    given = {
        "x": f["x"].reshape(BC, N), "conv_w": conv, "conv_p": cp, "out_w": ow, "ln_g": f["L0_attn_ln_gamma"],
        "ln_b": f["L0_attn_ln_beta"], "w_in": w_in, "gate_b": f["L0_attn_b_gate"].reshape(HG, 128).T,
        "w_fin": f["L0_attn_W_final"].T.reshape(HG, 128, C).transpose(1, 0, 2), "fin_b": f["L0_attn_b_final"],
        "experts": experts, "proj_w": f["L0_ffn_proj_w"].T, "proj_b": f["L0_ffn_proj_b"].reshape(E, 1),
        "scale": f["L0_ffn_scale"].reshape(C), "c_ident": ident, "c_sel": sel, "c_sum": sums, "c_pat": pat,
        "c_score": score, "c_bias": bias.astype(np.float32),
    }
    nc = bacc.Bacc("TRN2", target_bir_lowering=False, num_devices=1)
    arrays, args = {}, []
    for name in _ORDER:
        v = np.ascontiguousarray(given[name])
        arrays[f"in_{name}"] = v
        args.append(nc.dram_tensor(f"in_{name}", v.shape, mybir.dt.from_np(v.dtype), kind="ExternalInput").ap())
    args.append(nc.dram_tensor("out_0", (B, N, C), F32, kind="ExternalOutput").ap())
    build(nc, *args)
    r = run_bass_kernel_spmd(nc, [arrays], core_ids=[0])
    return r.results[0]["out_0"]
```
